# Optimizing a Trainium2 kernel written in Bass

```python
import numpy as np
import jax
import jax.numpy as jnp

def _softmax(x, axis=-1):
    return jax.nn.softmax(x, axis=axis)

def _gelu(x):
    return jax.nn.gelu(x, approximate=True)

def _silu(x):
    return jax.nn.silu(x)

def _sigmoid(x):
    return jax.nn.sigmoid(x)

def _layernorm(x, axis=-1, eps=1e-05):
    m = jnp.mean(x, axis=axis, keepdims=True)
    v = jnp.var(x, axis=axis, keepdims=True)
    return (x - m) / jnp.sqrt(v + eps)

def _scatter_add(tgt, idx, src, axis=0):
    return tgt.at[idx].add(src)

def _segment_sum(src, seg, n):
    return jax.ops.segment_sum(src, seg, n)
kernel_name = 'mk_seq_preln_d1_jaxref_r8_98aaf1'

def setup_inputs(seed: int=0):
    np.random.seed(seed)
    _w = jnp.asarray

    def _L0_attn_setup():
        import jax, jax.numpy as jnp
        import numpy as np
        N_HEAD = 16
        L_PARAM = 2

        def _build_sets(T, Lp):
            sets = []
            L = 2 ** Lp
            while L <= T:
                for i in range(T // L):
                    sets.append((i * L, (i + 1) * L - 1))
                L *= 2
            return np.asarray(sets, dtype=np.int32)

        def _get_slice(x_cum, l_idx, r_idx):
            r = x_cum[:, :, r_idx, :]
            l = x_cum[:, :, l_idx - 1, :] * (l_idx >= 1)[None, None, :, None]
            return r - l
        key = jax.random.key(seed)
        k1, k2, k3 = jax.random.split(key, 3)
        B, T, C = (2, 256, 128)
        x = jax.random.normal(k1, (B, T, C), dtype=jnp.float32)
        W_attn = jax.random.normal(k2, (3 * C, C), dtype=jnp.float32) * 0.02
        W_proj = jax.random.normal(k3, (C, C), dtype=jnp.float32) * 0.02
        return {'x': x, 'W_attn': W_attn, 'W_proj': W_proj}
    _L0_attn_in = _L0_attn_setup()

    def _L0_ffn_setup():
        import jax, jax.numpy as jnp
        import numpy as np
        HIDDEN = 128
        MOE_INTER = 64
        SHARED_INTER = 256
        N_EXPERTS = 32
        TOP_K = 6
        N_GROUP = 8
        TOPK_GROUP = 4
        ROUTED_SCALE = 2.5

        def _relu2(x):
            return jnp.square(jax.nn.relu(x))

        def _router(x, gate_w, e_bias):
            T = x.shape[0]
            logits = x.astype(jnp.float32) @ gate_w.astype(jnp.float32).T
            scores = jax.nn.sigmoid(logits)
            sc = scores + e_bias[None, :]
            g = sc.reshape(T, N_GROUP, N_EXPERTS // N_GROUP)
            group_scores = jax.lax.top_k(g, 2)[0].sum(-1)
            group_idx = jax.lax.top_k(group_scores, TOPK_GROUP)[1]
            group_mask = jnp.zeros_like(group_scores).at[jnp.arange(T)[:, None], group_idx].set(1.0)
            score_mask = jnp.repeat(group_mask, N_EXPERTS // N_GROUP, axis=1)
            masked = jnp.where(score_mask > 0, sc, 0.0)
            topk_idx = jax.lax.stop_gradient(jax.lax.top_k(masked, TOP_K)[1])
            topk_w = jnp.take_along_axis(scores, topk_idx, axis=1)
            topk_w = topk_w / (topk_w.sum(-1, keepdims=True) + 1e-20)
            topk_w = topk_w * ROUTED_SCALE
            return (topk_idx, topk_w)
        if __name__ == '__main__':
            out = reference(**setup_inputs())
            print(out.shape, out.dtype)
        key = jax.random.key(seed)
        ks = jax.random.split(key, 6)
        s = 0.02
        return {'hidden_states': jax.random.normal(ks[0], (2, 128, HIDDEN), jnp.float32), 'gate_w': jax.random.normal(ks[1], (N_EXPERTS, HIDDEN), jnp.float32) * s, 'e_bias': jnp.zeros((N_EXPERTS,), jnp.float32), 'up_w': jax.random.normal(ks[2], (N_EXPERTS, MOE_INTER, HIDDEN), jnp.float32) * s, 'down_w': jax.random.normal(ks[3], (N_EXPERTS, HIDDEN, MOE_INTER), jnp.float32) * s, 'shared_up_w': jax.random.normal(ks[4], (SHARED_INTER, HIDDEN), jnp.float32) * s, 'shared_down_w': jax.random.normal(ks[5], (HIDDEN, SHARED_INTER), jnp.float32) * s}
    _L0_ffn_in = _L0_ffn_setup()
    _d = {'L0_attn_x': _L0_attn_in['x'], 'L0_attn_W_attn': _L0_attn_in['W_attn'], 'L0_attn_W_proj': _L0_attn_in['W_proj'], 'L0_ffn_gate_w': _L0_ffn_in['gate_w'], 'L0_ffn_e_bias': _L0_ffn_in['e_bias'], 'L0_ffn_up_w': _L0_ffn_in['up_w'], 'L0_ffn_down_w': _L0_ffn_in['down_w'], 'L0_ffn_shared_up_w': _L0_ffn_in['shared_up_w'], 'L0_ffn_shared_down_w': _L0_ffn_in['shared_down_w']}
    _x0 = _d['L0_attn_x']
    _d['L0_attn_x'] = jax.random.normal(jax.random.fold_in(jax.random.key(seed), 1), (4, 1024, 128), dtype=_x0.dtype)
    del _x0
    return _d

def reference(L0_attn_x, L0_attn_W_attn, L0_attn_W_proj, L0_ffn_gate_w, L0_ffn_e_bias, L0_ffn_up_w, L0_ffn_down_w, L0_ffn_shared_up_w, L0_ffn_shared_down_w):

    def _L0_attn_ref(x, W_attn, W_proj):
        import jax, jax.numpy as jnp
        import numpy as np
        N_HEAD = 16
        L_PARAM = 2

        def _build_sets(T, Lp):
            sets = []
            L = 2 ** Lp
            while L <= T:
                for i in range(T // L):
                    sets.append((i * L, (i + 1) * L - 1))
                L *= 2
            return np.asarray(sets, dtype=np.int32)

        def _get_slice(x_cum, l_idx, r_idx):
            r = x_cum[:, :, r_idx, :]
            l = x_cum[:, :, l_idx - 1, :] * (l_idx >= 1)[None, None, :, None]
            return r - l
        B, T, C = x.shape
        nh, hs = (N_HEAD, C // N_HEAD)
        scale = 1.0 / np.sqrt(hs).astype(np.float32)
        qkv = x @ W_attn.T
        q, k, v = jnp.split(qkv, 3, axis=2)
        q = q.reshape(B, T, nh, hs).transpose(0, 2, 1, 3)
        k = k.reshape(B, T, nh, hs).transpose(0, 2, 1, 3)
        v = v.reshape(B, T, nh, hs).transpose(0, 2, 1, 3)
        k_cum = jnp.cumsum(k, axis=2)
        v_cum = jnp.cumsum(v, axis=2)
        sets = _build_sets(T, L_PARAM)
        l_idx = jnp.asarray(sets[:, 0])
        r_idx = jnp.asarray(sets[:, 1])
        K = _get_slice(k_cum, l_idx, r_idx)
        V = _get_slice(v_cum, l_idx, r_idx)
        t = jnp.arange(T)
        mask = t[:, None] >= r_idx[None, :]
        att_logits = jnp.einsum('bhtd,bhsd->bhts', q, K) * scale
        att_logits = jnp.where(mask[None, None], att_logits, -jnp.inf)
        Lmin = 2 ** L_PARAM
        tail_len = t % Lmin + 1
        l_tail = t - tail_len + 1
        K_tail = _get_slice(k_cum, l_tail, t)
        V_tail = _get_slice(v_cum, l_tail, t)
        att_tail = jnp.sum(q * K_tail, axis=-1) * scale
        logits = jnp.concatenate([att_logits, att_tail[..., None]], axis=-1)
        att = jax.nn.softmax(logits, axis=-1)
        out = jnp.einsum('bhts,bhsd->bhtd', att[..., :-1], V) + att[..., -1:] * V_tail
        out = out.transpose(0, 2, 1, 3).reshape(B, T, C)
        return out @ W_proj.T

    def _L0_ffn_ref(hidden_states, gate_w, e_bias, up_w, down_w, shared_up_w, shared_down_w):
        import jax, jax.numpy as jnp
        import numpy as np
        HIDDEN = 128
        MOE_INTER = 64
        SHARED_INTER = 256
        N_EXPERTS = 32
        TOP_K = 6
        N_GROUP = 8
        TOPK_GROUP = 4
        ROUTED_SCALE = 2.5

        def _relu2(x):
            return jnp.square(jax.nn.relu(x))

        def _router(x, gate_w, e_bias):
            T = x.shape[0]
            logits = x.astype(jnp.float32) @ gate_w.astype(jnp.float32).T
            scores = jax.nn.sigmoid(logits)
            sc = scores + e_bias[None, :]
            g = sc.reshape(T, N_GROUP, N_EXPERTS // N_GROUP)
            group_scores = jax.lax.top_k(g, 2)[0].sum(-1)
            group_idx = jax.lax.top_k(group_scores, TOPK_GROUP)[1]
            group_mask = jnp.zeros_like(group_scores).at[jnp.arange(T)[:, None], group_idx].set(1.0)
            score_mask = jnp.repeat(group_mask, N_EXPERTS // N_GROUP, axis=1)
            masked = jnp.where(score_mask > 0, sc, 0.0)
            topk_idx = jax.lax.stop_gradient(jax.lax.top_k(masked, TOP_K)[1])
            topk_w = jnp.take_along_axis(scores, topk_idx, axis=1)
            topk_w = topk_w / (topk_w.sum(-1, keepdims=True) + 1e-20)
            topk_w = topk_w * ROUTED_SCALE
            return (topk_idx, topk_w)
        if __name__ == '__main__':
            out = reference(**setup_inputs())
            print(out.shape, out.dtype)
        B, S, H = hidden_states.shape
        x = hidden_states.reshape(-1, H)
        T = x.shape[0]
        topk_idx, topk_w = _router(x, gate_w, e_bias)
        combine = jnp.zeros((T, N_EXPERTS), topk_w.dtype).at[jnp.arange(T)[:, None], topk_idx].add(topk_w)
        h = _relu2(jnp.einsum('th,eih->tei', x, up_w))
        h = h * combine[:, :, None]
        moe_out = jnp.einsum('tei,ehi->th', h, down_w)
        shared = _relu2(x @ shared_up_w.T) @ shared_down_w.T
        return (moe_out + shared).reshape(B, S, H)
    x = L0_attn_x
    x = x + _L0_attn_ref(_layernorm(x, axis=-1), L0_attn_W_attn, L0_attn_W_proj)
    x = x + _L0_ffn_ref(_layernorm(x, axis=-1), L0_ffn_gate_w, L0_ffn_e_bias, L0_ffn_up_w, L0_ffn_down_w, L0_ffn_shared_up_w, L0_ffn_shared_down_w)
    return x

_drawn_inputs = setup_inputs


def setup_inputs(seed=0):
    import zlib

    import numpy as np

    out = dict(_drawn_inputs(seed))
    spreads = {'L0_ffn_e_bias': (0.0, 0.76)}
    factors = {'L0_ffn_gate_w': 7.769,
     'L0_ffn_up_w': 6.093,
     'L0_ffn_down_w': 5.543,
     'L0_ffn_shared_up_w': 3.059,
     'L0_ffn_shared_down_w': 2.778}
    for name, (base, spread) in spreads.items():
        noise = np.random.default_rng([zlib.crc32(name.encode()), seed]).standard_normal(out[name].shape)
        drawn = base * np.exp(spread * noise) if base else spread * noise
        out[name] = jnp.asarray(drawn.astype(out[name].dtype))
    for name, factor in factors.items():
        out[name] = (out[name] * factor).astype(out[name].dtype)
    return out
```

```python
import concourse.bass as bass
from concourse import mybir
from contextlib import ExitStack

B, T, C = 4, 1024, 128
P = 128
NT = T // P
NH, HS = 16, 8
G, NG = 4, 4
NE, TOPK, NGRP, TOPG = 32, 6, 8, 4
GE = NE // NGRP
ROUTED_SCALE = 2.5
NCH = (NE * 64 + 256) // P
SCALE = 1.0 / float(HS) ** 0.5
BIG = 1e30
BLK = 64
NS = NT * BLK
WIN = 512

ROW_PART = 9 * HS
N_MASK_ROWS = 3
K_RAW = ROW_PART + N_MASK_ROWS
K_SUB = K_RAW + 3

MAX_UNITS = ([(i, h, 1) for i in (7, 6, 5, 4) for h in range(G)]
             + [(i, h, 2) for i in (3, 2) for h in (0, 2)] + [(1, 0, 4), (0, 0, 4)])
NMU = len(MAX_UNITS)
EXP_UNITS, PV_STEPS = [], []
for _w in range(T // WIN):
    for _c in range(2 * _w + 2):
        _full = _c < 2 * _w + 1
        _t0 = _w * WIN if _full else _c * 2 * P
        _n = WIN if _full else 2 * P
        for _h in ((0, 2) if _full else (0,)):
            EXP_UNITS.append((_w, _c, _h, 2 if _full else 4, _t0, _n))
        PV_STEPS.append((_w, _c, _t0, _n, len(EXP_UNITS)))
NEU, NPV = len(EXP_UNITS), len(PV_STEPS)
NPT = 4


def attention_order():
    maxes = []
    for g in range(NG):
        for n in range(NMU):
            maxes.append(("max", g, n))
            if g and n == 5:
                maxes.append(("mT", g - 1, 0))
        maxes.append(("mfin", g, 0))
    exps, pv, tail = [], [], []
    flat_steps = [(g, s) for g in range(NG) for s in range(NPV)]
    need = [g * NEU + PV_STEPS[s][4] for g, s in flat_steps]
    done = 0
    late = {}
    for n in range(NG * NEU + 8):
        evs = []
        if n < NG * NEU:
            evs.append(("exp", n // NEU, n % NEU))
        evs += late.pop(n, [])
        while done < len(need) and need[done] <= n - 1:
            g, s = flat_steps[done]
            evs.append(("pv", g, s))
            done += 1
            if s == NPV - 1 or PV_STEPS[s + 1][0] != PV_STEPS[s][0]:
                late.setdefault(n + 1, []).append(("oevac", g, PV_STEPS[s][0]))
                late.setdefault(n + 2, []).append(("oT", g, PV_STEPS[s][0]))
        exps.append(evs)
    order = []
    lead = NMU + 1 + 6 + 1
    order += maxes[:lead]
    rest = maxes[lead:]
    span = (NG - 1) * NEU - 7
    used = 0
    for n, evs in enumerate(exps):
        order += evs
        upto = min(len(rest), -(-len(rest) * (n + 1) // span))
        order += rest[used:upto]
        used = upto
        if n == span + 3:
            order.append(("mT", NG - 1, 0))
            order.append(("tail", 0, 0))
    return order


ORDER = attention_order()


class Chain:

    def __init__(self, eng, sem, per, spare):
        self.eng, self.sem, self.per, self.spare = eng, sem, per, spare

    def begin(self, b):
        self.b, self.n = b, 0

    def __call__(self, ins):
        self.n += 1
        ins.then_inc(self.sem, 1)
        self.eng.wait_ge(self.sem, self.b * self.per + self.n)

    def alone(self, ins):
        self(ins)
        self.eng.sem_inc(self.spare, 1)

    def end(self):
        assert self.n == self.per, (self.n, self.per)


def build(nc, x, w_qkv, w_proj, gate, e_bias, up, down, ident_c, head_sel_c, stair_t_c, stair_s_c,
          q_rows_c, k_rows_c, exp_sel_c, out):
    f32, bf16 = mybir.dt.float32, mybir.dt.bfloat16
    ALU, ACT, AX = mybir.AluOpType, mybir.ActivationFunctionType, mybir.AxisListType
    ctx = ExitStack()
    with ctx:
        def sb(name, shape, dt=f32):
            return ctx.enter_context(nc.sbuf_tensor(name, shape, dt))

        def sem(name):
            return ctx.enter_context(nc.semaphore(name))

        wqkv = sb("wqkv", [P, 3 * C])
        wproj = sb("wproj", [P, C])
        wgate = sb("wgate", [P, NE])
        bias = sb("bias", [P, NE])
        wup = sb("wup", [P, NCH * P])
        wdown = sb("wdown", [P, NCH, C])
        ident = sb("ident", [P, P])
        identb = sb("identb", [P, P], bf16)
        head_sel = sb("head_sel", [P, NH])
        stair_t = sb("stair_t", [P, BLK], bf16)
        stair_s = sb("stair_s", [P, 2 * P], bf16)
        exp_sel = sb("exp_sel", [3 * NE, 16, P], bf16)
        X = sb("X", [P, NT, C])
        stats = sb("stats", [P, NT, 6])
        mv = sb("mv", [P, NT, 2])
        var = sb("var", [P, NT])
        std = sb("std", [P, NT])
        rstd = sb("rstd", [P, NT])
        XN = sb("XN", [P, NT, C])
        XNT = sb("XNT", [P, T])
        QT = sb("QT", [P, T])
        TAIL = sb("TAIL", [P, 2, T // 4, 4])
        SUMS = sb("SUMS", [P, 2, NT, BLK])
        Qparts = sb("Qparts", [P, 3, T], bf16)
        Kparts = sb("Kparts", [P, 3, NS], bf16)
        qrem = sb("qrem", [P, T])
        krem = sb("krem", [P, NS])
        PROD = XNT
        QA = sb("QA", [K_SUB, NH, T], bf16)
        KA = sb("KA", [K_SUB, NH, NS], bf16)
        VA = sb("VA", [P, NS // P, NH, 32])
        VTL = sb("VTL", [P, NT, C])
        TLG = sb("TLG", [P, NT, NH])
        MXR = sb("MXR", [P, NG, NT, G])
        MALL = sb("MALL", [P, NG, G, NT])
        mrem = sb("mrem", [P, G * NT])
        MS = sb("MS", [P, 3, G * NT], bf16)
        MB = sb("MB", [3 * G * NT, P], bf16)
        PT = sb("PT", [P, NPT, G, WIN])
        OS = sb("OS", [P, WIN])
        ATT = sb("ATT", [P, NT, NH, HS + 1])
        TD = sb("TD", [P, NT, NH])
        ET = sb("ET", [P, NT, NH])
        VW = sb("VW", [P, NT, C])
        DEN = sb("DEN", [P, NT, NH])
        AO = VW
        X1 = sb("X1", [P, NT, C])
        XN2T = sb("XN2T", [P, T])
        ATTT = XN2T
        SCO = sb("SCO", [P, NT, NE])
        SCB = sb("SCB", [P, NT, NE])
        hi2 = sb("hi2", [P, 2, NT, NGRP, 2])
        grp = sb("grp", [P, NT, NGRP + 4])
        grpo = sb("grpo", [P, NT, NGRP + 4])
        top8 = sb("top8", [P, NT, 8])
        gmask = sb("gmask", [P, NT, NGRP])
        cand = sb("cand", [P, NT, NE + 2])
        cando = sb("cando", [P, NT, NE + 2])
        WSEL = sb("WSEL", [P, NT, NE])
        wsum = sb("wsum", [P, NT])
        wrem = sb("wrem", [P, NT, NE])
        CP = sb("CP", [P, NT, 3, NE], bf16)
        CT = sb("CT", [3 * NE, T], bf16)
        R, V, H = (PT[:, n, 0:3, :] for n in range(3))
        OT = sb("OT", [P, 2, WIN])
        Y = sb("Y", [P, 2, 4, C])

        st = ctx.enter_context(nc.psum_tensor("st", [P, 4, WIN], f32))
        mx = ctx.enter_context(nc.psum_tensor("mx", [P, 2, WIN], f32))
        om = ctx.enter_context(nc.psum_tensor("om", [P, 2, WIN], f32))
        misc, opsum = om[:, 0, :], om[:, 1, :]

        Qd = nc.dram_tensor("q_parts", [3, P, T], bf16, kind="Internal").ap()
        Kd = nc.dram_tensor("k_parts", [3, P, NS], bf16, kind="Internal").ap()

        s_w = sem("weights_loaded")
        s_x = sem("x_loaded")
        s_out = sem("out_stored")
        s_init = sem("constants_set")
        s_qd = sem("q_parts_stored")
        s_kd = sem("k_parts_stored")
        s_qa = sem("qa_loaded")
        s_ka = sem("ka_loaded")
        s_mrow = sem("max_rows_loaded")
        s_var1, s_std1, s_xn1 = sem("var1_ready"), sem("std1_ready"), sem("xn1_ready")
        s_pfill, s_pevac = sem("prep_bank_filled"), sem("prep_bank_evacuated")
        s_tails, s_sums, s_prod = sem("tails_ready"), sem("sums_ready"), sem("prod_ready")
        s_qsplit, s_ksplit = sem("q_split"), sem("k_split")
        s_maxin, s_maxed = sem("max_unit_filled"), sem("max_unit_reduced")
        s_msplit, s_mT, s_mb = sem("max_split"), sem("max_transposed"), sem("max_rows_ready")
        s_expin, s_exped = sem("exp_unit_filled"), sem("exp_unit_done")
        s_pv, s_oevac, s_oT, s_oext = sem("pv_done"), sem("o_evacuated"), sem("o_transposed"), sem("o_extracted")
        s_td, s_et = sem("tail_diff_ready"), sem("tail_exp_ready")
        s_ao, s_aT, s_aTe = sem("attn_out_ready"), sem("attn_transposed"), sem("attn_T_evacuated")
        s_proj, s_x1 = sem("projected"), sem("x1_ready")
        s_var2, s_std2, s_xn2 = sem("var2_ready"), sem("std2_ready"), sem("xn2_ready")
        s_x2T, s_x2e = sem("xn2_transposed"), sem("xn2_T_evacuated")
        s_rl, s_sg = sem("router_logits"), sem("router_scores")
        s_cp, s_cT, s_ce = sem("combine_ready"), sem("combine_transposed"), sem("combine_T_evacuated")
        s_up, s_bc, s_dn = sem("up_done"), sem("weights_broadcast"), sem("down_done")
        s_relu, s_vw, s_h = sem("relu_done"), sem("weighted"), sem("hidden_ready")
        s_dev, s_yT, s_y = sem("down_evacuated"), sem("y_transposed"), sem("y_ready")
        s_spare = sem("spare")
        s_cd1, s_cd2, s_cp1 = sem("dve_chain_prep"), sem("dve_chain_main"), sem("pool_chain_prep")

        N_WEIGHT_DMAS = 14
        FILLS = 12
        UNITS = 2 * NCH
        CHUNKS = [16, 17] + list(range(16))
        MAXN, EXPN, PVN = NG * NMU, NG * NEU, NG * NPV
        pos_max = lambda g, n: g * NMU + n
        pos_exp = lambda g, n: g * NEU + n
        pos_pv = lambda g, s: g * NPV + s

        PREP_AT = {0: ["ln_stats"], 3: ["ln_apply"], 5: ["f0"], 6: ["f1"], 7: ["f4"], 8: ["f5"], 9: ["f6"],
                   10: ["f7"], 11: ["f2", "tails"], 12: ["f3", "sums"], 13: ["ksplit"], 14: [], 15: ["qsplit"],
                   18: ["prod"], 19: ["f8"], 20: ["f9"], 21: ["f10"], 22: ["f11"]}
        PREP_ALL = [s for u in sorted(PREP_AT) for s in PREP_AT[u]]
        FILL_ORDER = [s for s in PREP_ALL if s[0] == "f"]
        fill_no = {s: n for n, s in enumerate(FILL_ORDER)}
        done_after = lambda s: fill_no[s] + 1

        block = ctx.enter_context(nc.Block())

        def batches(eng, body):
            with eng.Fori(0, B - 1) as b:
                body(b, False)
            body(B - 1, True)

        @block.sync
        def _(sp):
            def load_x(p):
                if not isinstance(p, int) or p:
                    sp.wait_ge(s_x1, 2 * p)
                src = x[bass.ds(p, 1)].rearrange("o (i p) c -> p (o i) c", p=P)
                sp.dma_start(X[:, :, :], src).then_inc(s_x, 16)

            def prep(p):
                sp.wait_ge(s_ksplit, p + 1)
                sp.dma_start(Kd.rearrange("a p s -> p a s"), Kparts[:, :, :]).then_inc(s_kd, 16)
                sp.wait_ge(s_qsplit, p + 1)
                sp.dma_start(Qd.rearrange("a p s -> p a s"), Qparts[:, :, :]).then_inc(s_qd, 16)
                sp.wait_ge(s_kd, 16 * p + 16)
                for i in range(3):
                    for j in range(3):
                        r = (3 * i + j) * HS
                        sp.dma_start(KA[r:r + HS, :, :], Kd[j].rearrange("(h d) s -> d h s", d=HS)).then_inc(s_ka, 16)
                sp.wait_ge(s_qd, 16 * p + 16)
                for i in range(3):
                    for j in range(3):
                        r = (3 * i + j) * HS
                        sp.dma_start(QA[r:r + HS, :, :], Qd[i].rearrange("(h d) s -> d h s", d=HS)).then_inc(s_qa, 16)

            load_x(0)
            for dst, src in ((wqkv, w_qkv), (ident, ident_c), (head_sel, head_sel_c), (stair_t, stair_t_c),
                             (stair_s, stair_s_c), (wproj, w_proj), (wgate, gate), (wup, up)):
                sp.dma_start(dst[:, :], src).then_inc(s_w, 16)
            sp.dma_start(bias[:, :], e_bias.rearrange("(o e) -> o e", o=1).partition_broadcast(P)
                         if False else e_bias.partition_broadcast(P)).then_inc(s_w, 16)
            sp.dma_start(wdown[:, :, :], down.rearrange("(k p) c -> p k c", p=P)).then_inc(s_w, 16)
            sp.dma_start(exp_sel[:, :, :], exp_sel_c).then_inc(s_w, 16)
            sp.dma_start(QA[ROW_PART:K_RAW, :, :], q_rows_c.unsqueeze(1).to_broadcast([N_MASK_ROWS, NH, T])).then_inc(s_w, 16)
            sp.dma_start(KA[ROW_PART:K_SUB, :, :], k_rows_c.unsqueeze(1).to_broadcast([K_SUB - ROW_PART, NH, NS])).then_inc(s_w, 16)
            prep(0)

            def body(b, last):
                for g in range(NG):
                    sp.wait_ge(s_mb, b * NG + g + 1)
                    for a in range(3):
                        sp.dma_start(QA[K_RAW + a:K_RAW + a + 1, G * g:G * g + G, :].rearrange("o h (i t) -> o (h i) t", t=P),
                                     MB[32 * a:32 * a + 32, :]).then_inc(s_mrow, 16)
                if not last:
                    load_x(b + 1)
                    prep(b + 1)
                for w in range(2):
                    sp.wait_ge(s_y, 2 * b + w + 1)
                    dst = out[bass.ds(b, 1), WIN * w:WIN * w + WIN].rearrange("o (i p) c -> p (o i) c", p=P)
                    sp.dma_start(dst, Y[:, w, :, :]).then_inc(s_out, 16)
            batches(sp, body)
            sp.wait_ge(s_out, 2 * 16 * B)
            sp.wait_ge(s_kd, 16 * B)
            sp.wait_ge(s_qd, 16 * B)

        @block.gpsimd
        def _(pool):
            chain = Chain(pool, s_cp1, 3, s_spare)
            pool.memset(VA[:, :, :, :], 0.0).then_inc(s_init, 1)
            pool.wait_ge(s_init, 1)
            pool.memset(VA[:, :, :, HS:HS + 1], 1.0).then_inc(s_init, 1)
            pool.memset(grp[:, :, 0:4], BIG).then_inc(s_init, 1)
            pool.memset(cand[:, :, 0:2], BIG).then_inc(s_init, 1)
            pool.memset(SUMS[:, :, 0, BLK - 1:BLK], 0.0).then_inc(s_init, 1)
            pool.wait_ge(s_w, 16 * (N_WEIGHT_DMAS - 1))
            pool.tensor_copy(identb[:, :], ident[:, :]).then_inc(s_init, 1)

            def qsplit(p):
                chain.begin(p)
                pool.wait_ge(s_pevac, p * FILLS + max(done_after("f2"), done_after("f3")))
                if not isinstance(p, int) or p:
                    pool.wait_ge(s_qd, 16 * p)
                pool.sem_inc(s_spare, 1)
                chain(pool.tensor_copy(Qparts[:, 0, :], QT[:, :]))
                chain.alone(pool.tensor_tensor(qrem[:, :], QT[:, :], Qparts[:, 0, :], ALU.subtract))
                chain(pool.tensor_copy(Qparts[:, 1, :], qrem[:, :]))
                pool.tensor_tensor(Qparts[:, 2, :], qrem[:, :], Qparts[:, 1, :], ALU.subtract).then_inc(s_qsplit, 1)
                chain.end()
            qsplit(0)

            def body(b, last):
                if not last:
                    qsplit(b + 1)
            batches(pool, body)

        @block.scalar
        def _(act):
            def prep_step(p, step):
                if step == "ln_apply":
                    act.wait_ge(s_var1, p + 1)
                    act.activation(std[:, :], var[:, :], ACT.Sqrt).then_inc(s_std1, 1)
                if step[0] != "f":
                    return
                n = fill_no[step]
                bank = om[:, n % 2, :]
                act.wait_ge(s_pfill, p * FILLS + n + 1)
                if step in ("f0", "f1"):
                    k = int(step[1])
                    ins = act.activation(XNT[:, WIN * k:WIN * k + WIN], bank, ACT.Copy)
                elif step in ("f2", "f3"):
                    k = int(step[1]) - 2
                    ins = act.activation(QT[:, WIN * k:WIN * k + WIN], bank, ACT.Copy)
                elif step in ("f4", "f5", "f6", "f7"):
                    k = int(step[1]) - 4
                    ins = act.activation(TAIL[:, k // 2, P * (k % 2):P * (k % 2) + P, :],
                                         bank.rearrange("p (n j) -> p n j", j=4), ACT.Copy)
                elif step == "f8":
                    ins = act.activation(VA[:, :, :, 0:HS], bank.rearrange("p (c h d) -> p c h d", c=4, d=HS), ACT.Copy)
                elif step in ("f9", "f10"):
                    k = int(step[1:]) - 9
                    ins = act.activation(VTL[:, 4 * k:4 * k + 4, :], bank.rearrange("p (i c) -> p i c", i=4), ACT.Copy)
                else:
                    ins = act.activation(TLG[:, :, :], bank[:, 0:P].rearrange("p (i h) -> p i h", i=NT), ACT.Copy)
                ins.then_inc(s_pevac, 1)

            def attend(b):
                for kind, g, n in ORDER:
                    if kind == "exp":
                        w, c, h0, nh, t0, nt = EXP_UNITS[n]
                        u = pos_exp(g, n)
                        step = [s for s in range(NPV) if PV_STEPS[s][:2] == (w, c)][0]
                        k = pos_pv(g, step)
                        act.wait_ge(s_expin, b * EXPN + u + 1)
                        if k >= NPT:
                            act.wait_ge(s_pv, b * PVN + k - NPT + 1)
                        src = st[:, 2 * (u % 2):2 * (u % 2) + 2, :].rearrange("p k (h t) -> p (k h) t", t=nt)
                        act.activation(PT[:, k % NPT, h0:h0 + nh, 0:nt], src, ACT.Exp, scale=SCALE).then_inc(s_exped, 1)
                    elif kind == "oevac":
                        act.wait_ge(s_pv, b * PVN + pos_pv(g, [1, 5][n]) + 1)
                        o = 2 * g + n
                        if o:
                            act.wait_ge(s_oT, b * 2 * NG + o)
                        act.activation(OS[:, :], opsum, ACT.Copy).then_inc(s_oevac, 1)
                    elif kind == "tail":
                        act.wait_ge(s_td, b + 1)
                        act.activation(ET[:, :, :], TD[:, :, :], ACT.Exp, scale=SCALE).then_inc(s_et, 1)

            def post(b):
                for w in range(2):
                    act.wait_ge(s_aT, 2 * b + w + 1)
                    act.activation(ATTT[:, WIN * w:WIN * w + WIN], st[:, w, :], ACT.Copy).then_inc(s_aTe, 1)
                act.wait_ge(s_var2, b + 1)
                act.activation(std[:, :], var[:, :], ACT.Sqrt).then_inc(s_std2, 1)
                for w in range(2):
                    act.wait_ge(s_x2T, 2 * b + w + 1)
                    act.activation(XN2T[:, WIN * w:WIN * w + WIN], mx[:, w, :], ACT.Copy).then_inc(s_x2e, 1)
                act.wait_ge(s_rl, b + 1)
                act.activation(SCO[:, :, :], opsum[:, 0:NT * NE].rearrange("p (i e) -> p i e", i=NT), ACT.Sigmoid).then_inc(s_sg, 1)

            def down_evac(b, w):
                act.wait_ge(s_dn, b * UNITS + NCH * (w + 1))
                act.activation(OT[:, w, :], mx[:, w, :], ACT.Copy).then_inc(s_dev, 1)

            def ffn(b, last):
                for u in range(UNITS):
                    act.wait_ge(s_up, b * UNITS + u + 1)
                    if u >= 3:
                        act.wait_ge(s_h, b * UNITS + u - 2)
                    act.activation(R[:, u % 3, :], st[:, u % 2, :], ACT.Relu).then_inc(s_relu, 1)
                    if u == 1:
                        act.wait_ge(s_cT, b + 1)
                        act.activation(CT[:, :], misc.bitcast(bf16)[0:3 * NE, :], ACT.Copy).then_inc(s_ce, 1)
                    if u == NCH + 3:
                        down_evac(b, 0)
                    if not last:
                        for step in PREP_AT.get(u, []):
                            prep_step(b + 1, step)
                down_evac(b, 1)

            act.wait_ge(s_init, 6)
            for step in PREP_ALL:
                prep_step(0, step)

            def body(b, last):
                attend(b)
                post(b)
                ffn(b, last)
            batches(act, body)

        @block.tensor
        def _(pe):
            def prep_step(p, step):
                if step[0] != "f":
                    return
                n = fill_no[step]
                bank = om[:, n % 2, :]
                if n >= 2:
                    pe.wait_ge(s_pevac, p * FILLS + n - 1)
                if step in ("f0", "f1"):
                    k = int(step[1])
                    pe.wait_ge(s_xn1, p * NT + 4 * k + 4)
                    for i in range(4):
                        ins = pe.transpose(bank[:, P * i:P * i + P], XN[:, 4 * k + i, :], ident[:, :])
                elif step in ("f2", "f3", "f4", "f5", "f6", "f7"):
                    k = int(step[1]) - 2
                    pe.wait_ge(s_pevac, p * FILLS + done_after("f1"))
                    ins = pe.matmul(bank, wqkv[:, C * (k // 2):C * (k // 2) + C],
                                    XNT[:, WIN * (k % 2):WIN * (k % 2) + WIN], start=True, stop=True)
                elif step == "f8":
                    pe.wait_ge(s_sums, p + 1)
                    for c in range(4):
                        ins = pe.transpose(bank[:, P * c:P * c + P],
                                           SUMS[:, 1, 2 * c:2 * c + 2, :].rearrange("p a s -> p (a s)"), ident[:, :])
                elif step in ("f9", "f10"):
                    k = int(step[1:]) - 9
                    pe.wait_ge(s_tails, p + 1)
                    for i in range(4):
                        v = TAIL[:, 1, 32 * (4 * k + i):32 * (4 * k + i) + 32, :].rearrange("p n j -> p (n j)")
                        ins = pe.transpose(bank[:, P * i:P * i + P], v, ident[:, :])
                else:
                    pe.wait_ge(s_prod, p + 1)
                    for i in range(NT):
                        ins = pe.matmul(bank[:, NH * i:NH * i + NH], PROD[:, P * i:P * i + P], head_sel[:, :],
                                        start=True, stop=True)
                ins.then_inc(s_pfill, 1)

            def attend(b):
                pe.wait_ge(s_ka, (b + 1) * 9 * 16)
                pe.wait_ge(s_qa, (b + 1) * 9 * 16)
                misc_use, first_o, first_max = 0, True, 0
                for kind, g, n in ORDER:
                    if kind == "max":
                        i, h0, nh = MAX_UNITS[n]
                        u = pos_max(g, n)
                        if u >= 2:
                            pe.wait_ge(s_maxed, b * MAXN + u - 1)
                        elif not isinstance(b, int) or b:
                            pe.wait_ge(s_y, 2 * b)
                        ns = BLK * (i + 1)
                        for k in range(nh):
                            h = G * g + h0 + k
                            o = mx[:, u % 2, ns * k:ns * k + ns]
                            pe.matmul(o, QA[0:K_RAW, h, P * i:P * i + P], KA[0:K_RAW, h, 0:ns],
                                      start=True, stop=False, skip_group_check=True)
                            ins = pe.matmul(o[:, ns - BLK:ns], identb[:, :], stair_t[:, :],
                                            start=False, stop=True, skip_group_check=True)
                        ins.then_inc(s_maxin, 1)
                    elif kind == "mT":
                        pe.wait_ge(s_msplit, b * NG + g + 1)
                        if misc_use:
                            pe.wait_ge(s_oext, b * 3 * NG + misc_use)
                        misc_use += 1
                        pe.transpose(misc.bitcast(bf16)[0:3 * G * NT, 0:P], MS[:, :, :].rearrange("p a m -> p (a m)"),
                                     identb[:, :]).then_inc(s_mT, 1)
                    elif kind == "exp":
                        w, c, h0, nh, t0, nt = EXP_UNITS[n]
                        u = pos_exp(g, n)
                        if n == 0:
                            pe.wait_ge(s_mrow, b * NG * 48 + 48 * (g + 1))
                        if u >= 2:
                            pe.wait_ge(s_exped, b * EXPN + u - 1)
                        elif not isinstance(b, int) or b:
                            pe.wait_ge(s_relu, b * UNITS)
                            pe.wait_ge(s_vw, b * 32)
                        for k in range(nh):
                            h = G * g + h0 + k
                            o = st[:, 2 * (u % 2) + k * nt // WIN, (k * nt) % WIN:(k * nt) % WIN + nt]
                            diag = c // 2 == w
                            pe_in = pe.matmul(o, KA[0:K_SUB, h, P * c:P * c + P], QA[0:K_SUB, h, t0:t0 + nt],
                                              start=True, stop=not diag, skip_group_check=True)
                            if diag:
                                pe_in = pe.matmul(o[:, 0:2 * P], identb[:, :], stair_s[:, :],
                                                  start=False, stop=True, skip_group_check=True)
                        pe_in.then_inc(s_expin, 1)
                    elif kind == "pv":
                        w, c, t0, nt, need = PV_STEPS[n]
                        k = pos_pv(g, n)
                        pe.wait_ge(s_exped, b * EXPN + pos_exp(g, need))
                        o = 2 * g + w
                        if c == 0 and o:
                            pe.wait_ge(s_oevac, b * 2 * NG + o)
                        for h in range(G):
                            ins = pe.matmul(opsum[32 * h:32 * h + 32, t0 - WIN * w:t0 - WIN * w + nt],
                                            VA[:, c, G * g + h, :], PT[:, k % NPT, h, 0:nt],
                                            start=(c == 0), stop=(c == 2 * w + 1), skip_group_check=True)
                        ins.then_inc(s_pv, 1)
                    elif kind == "oT":
                        pe.wait_ge(s_oevac, b * 2 * NG + 2 * g + n + 1)
                        if misc_use:
                            pe.wait_ge(s_oext, b * 3 * NG + misc_use)
                        misc_use += 1
                        for i in range(4):
                            ins = pe.transpose(misc[:, P * i:P * i + P], OS[:, P * i:P * i + P], ident[:, :])
                        ins.then_inc(s_oT, 1)

            def post(b):
                pe.wait_ge(s_ao, b + 1)
                pe.wait_ge(s_exped, (b + 1) * EXPN)
                for w in range(2):
                    for i in range(4):
                        ins = pe.transpose(st[:, w, P * i:P * i + P], AO[:, 4 * w + i, :], ident[:, :])
                    ins.then_inc(s_aT, 1)
                for w in range(2):
                    pe.wait_ge(s_aTe, 2 * b + w + 1)
                    for i in range(4):
                        t0 = P * (4 * w + i)
                        ins = pe.matmul(st[:, 2 + w, P * i:P * i + P], ATTT[:, t0:t0 + P], wproj[:, :], start=True, stop=True)
                    ins.then_inc(s_proj, 1)
                pe.wait_ge(s_maxed, (b + 1) * MAXN)
                for w in range(2):
                    pe.wait_ge(s_xn2, b * NT + 4 * w + 4)
                    for i in range(4):
                        ins = pe.transpose(mx[:, w, P * i:P * i + P], XN[:, 4 * w + i, :], ident[:, :])
                    ins.then_inc(s_x2T, 1)
                pe.wait_ge(s_x2e, 2 * b + 2)
                pe.wait_ge(s_oevac, (b + 1) * 2 * NG)
                for i in range(NT):
                    ins = pe.matmul(opsum[:, NE * i:NE * i + NE], XN2T[:, P * i:P * i + P], wgate[:, :], start=True, stop=True)
                ins.then_inc(s_rl, 1)

            def y_transpose(b, w):
                pe.wait_ge(s_dev, 2 * b + w + 1)
                for i in range(4):
                    ins = pe.transpose(mx[:, w, P * i:P * i + P], OT[:, w, P * i:P * i + P], ident[:, :])
                ins.then_inc(s_yT, 1)

            def ffn(b, last):
                routed = 0
                for v in range(UNITS + 2):
                    if v < UNITS:
                        w, k = v // NCH, CHUNKS[v % NCH]
                        if v == 0:
                            pe.wait_ge(s_x1, 2 * b + 2)
                        if v >= 2:
                            pe.wait_ge(s_relu, b * UNITS + v - 1)
                        pe.matmul(st[:, v % 2, :], wup[:, P * k:P * k + P], XN2T[:, WIN * w:WIN * w + WIN],
                                  start=True, stop=True).then_inc(s_up, 1)
                        if k < 16:
                            if routed == 0:
                                pe.wait_ge(s_ce, b + 1)
                            if routed >= 2:
                                pe.wait_ge(s_vw, b * 32 + routed - 1)
                            pe.matmul(st[:, 2 + routed % 2, :], exp_sel[:, k, :], CT[:, WIN * w:WIN * w + WIN],
                                      start=True, stop=True).then_inc(s_bc, 1)
                            routed += 1
                        if v == 1:
                            pe.wait_ge(s_cp, b + 1)
                            pe.wait_ge(s_oext, (b + 1) * 3 * NG)
                            for i in range(NT):
                                ins = pe.transpose(misc.bitcast(bf16)[0:3 * NE, P * i:P * i + P],
                                                   CP[:, i, :, :].rearrange("p a e -> p (a e)"), identb[:, :])
                            ins.then_inc(s_cT, 1)
                    if v >= 2:
                        d = v - 2
                        w, n = d // NCH, d % NCH
                        if d == 0:
                            pe.wait_ge(s_x2e, 2 * b + 2)
                        pe.wait_ge(s_h, b * UNITS + d + 1)
                        pe.matmul(mx[:, w, :], wdown[:, CHUNKS[n], :], H[:, d % 3, :],
                                  start=(n == 0), stop=(n == NCH - 1)).then_inc(s_dn, 1)
                    if v == NCH + 5:
                        y_transpose(b, 0)
                    if not last and v < UNITS:
                        for step in PREP_AT.get(v, []):
                            if step == FILL_ORDER[0]:
                                pe.wait_ge(s_ce, b + 1)
                            if step == FILL_ORDER[1]:
                                pe.wait_ge(s_sg, b + 1)
                            prep_step(b + 1, step)
                y_transpose(b, 1)

            pe.wait_ge(s_w, 16 * (N_WEIGHT_DMAS - 1))
            pe.wait_ge(s_init, 6)
            for step in PREP_ALL:
                prep_step(0, step)

            def body(b, last):
                attend(b)
                post(b)
                ffn(b, last)
            def body_(b, last):
                pe.wait_ge(s_pevac, (b + 1) * FILLS)
                body(b, last)
            batches(pe, body_)

        @block.vector
        def _(dve):
            chain1 = Chain(dve, s_cd1, 17, s_spare)
            chain2 = Chain(dve, s_cd2, 48, s_spare)

            def ln_stats(src, chain, s_var):
                for i in range(NT):
                    ins = dve.bn_stats(stats[:, i, :], src[:, i, :])
                chain.alone(ins)
                for i in range(NT):
                    ins = dve.bn_aggr(mv[:, i, :], stats[:, i, :])
                chain(ins)
                dve.tensor_scalar(var[:, :], mv[:, :, 1], 1e-5, None, ALU.add).then_inc(s_var, 1)

            def ln_apply(src, chain, s_std, v, s_xn):
                dve.wait_ge(s_std, v)
                chain(dve.reciprocal(rstd[:, :], std[:, :]))
                for i in range(NT):
                    dve.tensor_scalar(XN[:, i, :], src[:, i, :], mv[:, i, 0:1], rstd[:, i:i + 1],
                                      ALU.subtract, ALU.mult).then_inc(s_xn, 1)

            def prep_step(p, step):
                if step == "ln_stats":
                    chain1.begin(p)
                    dve.wait_ge(s_x, 16 * p + 16)
                    ln_stats(X, chain1, s_var1)
                elif step == "ln_apply":
                    ln_apply(X, chain1, s_std1, p + 1, s_xn1)
                elif step == "tails":
                    dve.wait_ge(s_pevac, p * FILLS + max(done_after(s) for s in ("f4", "f5", "f6", "f7")))
                    for j in (1, 2):
                        chain1(dve.tensor_tensor(TAIL[:, :, :, j], TAIL[:, :, :, j], TAIL[:, :, :, j - 1], ALU.add))
                    dve.tensor_tensor(TAIL[:, :, :, 3], TAIL[:, :, :, 3], TAIL[:, :, :, 2], ALU.add).then_inc(s_tails, 1)
                elif step == "sums":
                    dve.wait_ge(s_tails, p + 1)
                    chain1(dve.tensor_copy(SUMS[:, :, :, 0:32], TAIL[:, :, :, 3].rearrange("p a (i s) -> p a i s", i=NT)))
                    at, n = 0, 32
                    while n > 1:
                        pair = SUMS[:, :, :, at:at + n].rearrange("p a i (s two) -> p a i s two", two=2)
                        chain1(dve.tensor_tensor(SUMS[:, :, :, at + n:at + n + n // 2], pair[:, :, :, :, 0],
                                                 pair[:, :, :, :, 1], ALU.add))
                        at, n = at + n, n // 2
                    half = SUMS[:, :, :, :].rearrange("p a (i two) s -> p a i two s", two=2)
                    L = BLK - 1
                    chain1(dve.tensor_tensor(half[:, :, :, 1, L], half[:, :, :, 0, L - 1], half[:, :, :, 1, L - 1], ALU.add))
                    for a in (0, 4):
                        chain1(dve.tensor_tensor(SUMS[:, :, a + 2, L], SUMS[:, :, a + 1, L], SUMS[:, :, a + 3, L], ALU.add))
                    dve.tensor_tensor(SUMS[:, :, 4, L], SUMS[:, :, 2, L], SUMS[:, :, 6, L], ALU.add).then_inc(s_sums, 1)
                elif step == "ksplit":
                    dve.wait_ge(s_sums, p + 1)
                    if not isinstance(p, int) or p:
                        dve.wait_ge(s_kd, 16 * p)
                    K = SUMS[:, 0, :, :].rearrange("p i s -> p (i s)")
                    chain1(dve.tensor_copy(Kparts[:, 0, :], K))
                    chain1(dve.tensor_tensor(krem[:, :], K, Kparts[:, 0, :], ALU.subtract))
                    chain1(dve.tensor_copy(Kparts[:, 1, :], krem[:, :]))
                    dve.tensor_tensor(Kparts[:, 2, :], krem[:, :], Kparts[:, 1, :], ALU.subtract).then_inc(s_ksplit, 1)
                elif step == "prod":
                    dve.wait_ge(s_pevac, p * FILLS + max(done_after("f2"), done_after("f3")))
                    dve.tensor_tensor(PROD[:, :], QT[:, :], TAIL[:, 0, :, :].rearrange("p n j -> p (n j)"),
                                      ALU.mult).then_inc(s_prod, 1)
                    chain1.end()

            def attend(b):
                for kind, g, n in ORDER:
                    if kind == "max":
                        i, h0, nh = MAX_UNITS[n]
                        u = pos_max(g, n)
                        ns = BLK * (i + 1)
                        dve.wait_ge(s_maxin, b * MAXN + u + 1)
                        dve.reduce_max(MXR[:, g, i, h0:h0 + nh], mx[:, u % 2, 0:ns * nh].rearrange("p (h s) -> p h s", s=ns),
                                       AX.X).then_inc(s_maxed, 1)
                    elif kind == "mfin":
                        dve.wait_ge(s_maxed, b * MAXN + pos_max(g, NMU - 1) + 1)
                        if g == 0:
                            dve.wait_ge(s_pevac, (b + 1) * FILLS)
                        M = MALL[:, g, :, :].rearrange("p h i -> p (h i)")
                        chain2(dve.tensor_tensor(MALL[:, g, :, :], MXR[:, g, :, :].rearrange("p i h -> p h i"),
                                                 TLG[:, :, G * g:G * g + G].rearrange("p i h -> p h i"), ALU.max))
                        if g:
                            dve.wait_ge(s_mT, b * NG + g)
                        chain2(dve.tensor_copy(MS[:, 0, :], M))
                        chain2(dve.tensor_tensor(mrem[:, :], M, MS[:, 0, :], ALU.subtract))
                        chain2(dve.tensor_copy(MS[:, 1, :], mrem[:, :]))
                        dve.tensor_tensor(MS[:, 2, :], mrem[:, :], MS[:, 1, :], ALU.subtract).then_inc(s_msplit, 1)
                    elif kind == "mT":
                        dve.wait_ge(s_mT, b * NG + g + 1)
                        if g:
                            dve.wait_ge(s_mrow, b * NG * 48 + 48 * g)
                        elif not isinstance(b, int) or b:
                            dve.wait_ge(s_mrow, b * NG * 48)
                        dve.tensor_copy(MB[:, :], misc.bitcast(bf16)[0:3 * G * NT, 0:P]).then_inc(s_mb, 1)
                        dve.wait_ge(s_mb, b * NG + g + 1)
                        dve.engine_nop().then_inc(s_oext, 1) if False else dve.sem_inc(s_oext, 1)
                    elif kind == "tail":
                        for g2 in range(NG):
                            ins = dve.tensor_tensor(TD[:, :, G * g2:G * g2 + G], TLG[:, :, G * g2:G * g2 + G],
                                                    MALL[:, g2, :, :].rearrange("p h i -> p i h"), ALU.subtract)
                        ins.then_inc(s_td, 1)
                    elif kind == "oT":
                        dve.wait_ge(s_oT, b * 2 * NG + 2 * g + n + 1)
                        dve.tensor_copy(ATT[:, 4 * n:4 * n + 4, G * g:G * g + G, :],
                                        misc.rearrange("p (i h d) -> p i h d", i=4, h=G)[:, :, :, 0:HS + 1]).then_inc(s_oext, 1)

            def post(b):
                dve.wait_ge(s_et, b + 1)
                heads = lambda t: t.rearrange("p i (h d) -> p (i h) d", d=HS)
                flat = lambda t: t.rearrange("p i h -> p (i h)").unsqueeze(2).to_broadcast([P, NT * NH, HS])
                chain2(dve.tensor_tensor(heads(VW[:, :, :]), heads(VTL[:, :, :]), flat(ET[:, :, :]), ALU.mult))
                dve.wait_ge(s_oext, (b + 1) * 3 * NG)
                chain2(dve.tensor_tensor(DEN[:, :, :], ATT[:, :, :, HS], ET[:, :, :], ALU.add))
                chain2(dve.reciprocal(DEN[:, :, :], DEN[:, :, :]))
                chain2(dve.tensor_tensor(heads(VW[:, :, :]), heads(VW[:, :, :]),
                                         ATT[:, :, :, 0:HS].rearrange("p i h d -> p (i h) d"), ALU.add))
                dve.tensor_tensor(heads(AO[:, :, :]), heads(VW[:, :, :]), flat(DEN[:, :, :]), ALU.mult).then_inc(s_ao, 1)
                for w in range(2):
                    dve.wait_ge(s_proj, 2 * b + w + 1)
                    dve.tensor_tensor(X1[:, 4 * w:4 * w + 4, :], st[:, 2 + w, :].rearrange("p (i c) -> p i c", i=4),
                                      X[:, 4 * w:4 * w + 4, :], ALU.add).then_inc(s_x1, 1)
                dve.wait_ge(s_x1, 2 * b + 2)
                ln_stats(X1, chain2, s_var2)
                ln_apply(X1, chain2, s_std2, b + 1, s_xn2)
                router(b)

            def router(b):
                dve.wait_ge(s_sg, b + 1)
                grid = lambda t: t.rearrange("p i e -> p (i e)")
                chain2(dve.tensor_tensor(SCB[:, :, :], SCO[:, :, :], bias[:, :].unsqueeze(1).to_broadcast([P, NT, NE]), ALU.add))
                four = SCB[:, :, :].rearrange("p i (g two k) -> p (i g) two k", g=NGRP, two=2)
                for k, op in ((0, ALU.max), (1, ALU.min)):
                    chain2(dve.tensor_tensor(hi2[:, k, :, :, :].rearrange("p i g k -> p (i g) k"), four[:, :, 0, :], four[:, :, 1, :], op))
                lo = hi2[:, 1, :, :, :].rearrange("p i g k -> p (i g) k")
                hi = hi2[:, 0, :, :, :].rearrange("p i g k -> p (i g) k")
                t1 = wrem[:, 0, :].rearrange("p e -> p e")
                a = wrem[:, :, 0:NGRP]
                c2 = wrem[:, :, NGRP:2 * NGRP]
                d = wrem[:, :, 2 * NGRP:3 * NGRP]
                hv = hi2[:, 0, :, :, :]
                lv = hi2[:, 1, :, :, :]
                chain2(dve.tensor_tensor(a, hv[:, :, :, 0], hv[:, :, :, 1], ALU.max))
                chain2(dve.tensor_tensor(c2, hv[:, :, :, 0], hv[:, :, :, 1], ALU.min))
                chain2(dve.tensor_tensor(d, lv[:, :, :, 0], lv[:, :, :, 1], ALU.max))
                chain2(dve.tensor_tensor(c2, c2, d, ALU.max))
                chain2.alone(dve.tensor_tensor(grp[:, :, 4:], a, c2, ALU.add))
                for i in range(NT):
                    ins = dve.max(top8[:, i, :], grp[:, i, :])
                chain2.alone(ins)
                for i in range(NT):
                    ins = dve.match_replace(grpo[:, i, :], top8[:, i, :], grp[:, i, :], -3.0 * BIG)
                chain2(ins)
                chain2(dve.tensor_tensor(gmask[:, :, :], grpo[:, :, 4:], grp[:, :, 4:], ALU.not_equal))
                chain2(dve.tensor_tensor(WSEL[:, :, :].rearrange("p i (g k) -> p (i g) k", k=GE),
                                         SCB[:, :, :].rearrange("p i (g k) -> p (i g) k", k=GE),
                                         gmask[:, :, :].rearrange("p i g -> p (i g)").unsqueeze(2).to_broadcast([P, NT * NGRP, GE]), ALU.mult))
                chain2.alone(dve.tensor_scalar(cand[:, :, 2:], WSEL[:, :, :], 0.0, None, ALU.add))
                for i in range(NT):
                    ins = dve.max(top8[:, i, :], cand[:, i, :])
                chain2.alone(ins)
                for i in range(NT):
                    ins = dve.match_replace(cando[:, i, :], top8[:, i, :], cand[:, i, :], -3.0 * BIG)
                chain2(ins)
                chain2(dve.tensor_tensor(WSEL[:, :, :], cando[:, :, 2:], cand[:, :, 2:], ALU.not_equal))
                chain2(dve.tensor_tensor(WSEL[:, :, :], WSEL[:, :, :], SCO[:, :, :], ALU.mult))
                chain2(dve.reduce_sum(wsum[:, :], WSEL[:, :, :], AX.X))
                chain2(dve.tensor_scalar(wsum[:, :], wsum[:, :], 1e-20, None, ALU.add))
                chain2(dve.reciprocal(wsum[:, :], wsum[:, :]))
                chain2(dve.tensor_tensor(WSEL[:, :, :], WSEL[:, :, :], wsum[:, :].unsqueeze(2).to_broadcast([P, NT, NE]), ALU.mult))
                chain2(dve.tensor_scalar(WSEL[:, :, :], WSEL[:, :, :], ROUTED_SCALE, None, ALU.mult))
                chain2(dve.tensor_copy(CP[:, :, 0, :], WSEL[:, :, :]))
                chain2(dve.tensor_tensor(wrem[:, :, :], WSEL[:, :, :], CP[:, :, 0, :], ALU.subtract))
                chain2(dve.tensor_copy(CP[:, :, 1, :], wrem[:, :, :]))
                dve.tensor_tensor(CP[:, :, 2, :], wrem[:, :, :], CP[:, :, 1, :], ALU.subtract).then_inc(s_cp, 1)

            def finish(b, w):
                dve.wait_ge(s_yT, 2 * b + w + 1)
                if not isinstance(b, int) or b:
                    dve.wait_ge(s_out, 32 * b)
                dve.tensor_tensor(Y[:, w, :, :], mx[:, w, :].rearrange("p (i c) -> p i c", i=4),
                                  X1[:, 4 * w:4 * w + 4, :], ALU.add).then_inc(s_y, 1)

            def ffn(b, last):
                routed = 0
                for v in range(UNITS + 1):
                    if v < UNITS:
                        k = CHUNKS[v % NCH]
                        dve.wait_ge(s_relu, b * UNITS + v + 1)
                        if k < 16:
                            dve.wait_ge(s_bc, b * 32 + routed + 1)
                            dve.tensor_tensor(V[:, v % 3, :], R[:, v % 3, :], st[:, 2 + routed % 2, :], ALU.mult).then_inc(s_vw, 1)
                            routed += 1
                    if v:
                        u = v - 1
                        k = CHUNKS[u % NCH]
                        if u >= 3:
                            dve.wait_ge(s_dn, b * UNITS + u - 2)
                        if k < 16:
                            dve.wait_ge(s_vw, b * 32 + (u // NCH) * 16 + (u % NCH) - 1)
                            src = V
                        else:
                            src = R
                        dve.tensor_tensor(H[:, u % 3, :], src[:, u % 3, :], R[:, u % 3, :], ALU.mult).then_inc(s_h, 1)
                    if v == NCH + 6:
                        finish(b, 0)
                    if not last and v < UNITS:
                        for step in PREP_AT.get(v, []):
                            prep_step(b + 1, step)
                finish(b, 1)

            dve.wait_ge(s_init, 6)
            dve.wait_ge(s_w, 16 * (N_WEIGHT_DMAS - 1))
            for step in PREP_ALL:
                prep_step(0, step)

            def body(b, last):
                chain2.begin(b)
                attend(b)
                post(b)
                chain2.end()
                ffn(b, last)
            batches(dve, body)


_INS = ["x", "w_qkv", "w_proj", "gate", "e_bias", "up", "down", "ident", "head_sel", "stair_t", "stair_s",
        "q_rows", "k_rows", "exp_sel"]


def layout(i):
    import numpy as np
    from concourse import mybir
    b16 = mybir.dt.np(mybir.dt.bfloat16)
    d = {k: np.asarray(v) for k, v in i.items()}
    up = np.concatenate([d["L0_ffn_up_w"].reshape(NE * 64, C), d["L0_ffn_shared_up_w"]], 0)
    down = np.concatenate([d["L0_ffn_down_w"].transpose(0, 2, 1).reshape(NE * 64, C), d["L0_ffn_shared_down_w"].T], 0)
    last = []
    n, size = 32, 4
    while n >= 1:
        last += [size * (k + 1) - 1 for k in range(n)]
        n, size = n // 2, size * 2
    last = np.array(last + [P - 1])
    t = np.arange(2 * P)
    stair_t = np.where(last[None, :] > t[:P, None], -BIG, 0.0)
    last2 = np.concatenate([last, last + P])
    stair_s = np.where(last2[:, None] > t[None, :], -BIG, 0.0)
    tt = np.arange(T)
    q_rows = np.stack([tt >= 0, tt < 511, tt < 1023]).astype(np.float32)
    k_rows = np.zeros((K_SUB - ROW_PART, NS), np.float32)
    k_rows[0, BLK - 1] = -BIG
    k_rows[1, 2 * BLK + BLK - 1] = -BIG
    k_rows[2, [4 * BLK + BLK - 1, 6 * BLK + BLK - 1]] = -BIG
    k_rows[3:] = -1.0
    head_sel = np.repeat(np.eye(NH, dtype=np.float32), HS, 0)
    exp_sel = np.zeros((3, NE, 16, P), np.float32)
    for e in range(NE):
        exp_sel[:, e, e // 2, 64 * (e % 2):64 * (e % 2) + 64] = 1.0
    return {
        "x": d["L0_attn_x"], "w_qkv": d["L0_attn_W_attn"].T, "w_proj": d["L0_attn_W_proj"].T,
        "gate": d["L0_ffn_gate_w"].T, "e_bias": d["L0_ffn_e_bias"], "up": up.T, "down": down,
        "ident": np.eye(P, dtype=np.float32), "head_sel": head_sel, "stair_t": stair_t.astype(b16),
        "stair_s": stair_s.astype(b16), "q_rows": q_rows.astype(b16), "k_rows": k_rows.astype(b16),
        "exp_sel": exp_sel.reshape(3 * NE, 16, P).astype(b16),
    }


def kernel(**inputs):
    import numpy as _np
    import concourse.bacc as _bacc
    from concourse import mybir as _mybir
    from concourse.bass_utils import run_bass_kernel_spmd as _run

    nc = _bacc.Bacc("TRN2", target_bir_lowering=False, num_devices=1)
    laid = layout(inputs)
    arrays, args = {}, []
    for name in _INS:
        a = _np.ascontiguousarray(laid[name])
        arrays[f"in_{name}_dram"] = a
        args.append(nc.dram_tensor(f"in_{name}_dram", a.shape, _mybir.dt.from_np(a.dtype), kind="ExternalInput").ap())
    args.append(nc.dram_tensor("out_0_dram", (B, T, C), _mybir.dt.float32, kind="ExternalOutput").ap())
    build(nc, *args)
    r = _run(nc, [arrays], core_ids=[0])
    return r.results[0]["out_0_dram"]
```

```python
import concourse.bass as bass
from concourse import mybir
from contextlib import ExitStack

B, T, C = 4, 1024, 128
P = 128
NT = T // P
NH, HS = 16, 8
G, NG = 4, 4
NE, TOPK, NGRP, TOPG = 32, 6, 8, 4
GE = NE // NGRP
ROUTED_SCALE = 2.5
NCH = (NE * 64 + 256) // P
SCALE = 1.0 / float(HS) ** 0.5
BIG = 1e30
BLK = 64
NS = NT * BLK
WIN = 512

N_STAIR = 2 * (P // 4)
PART_PAIRS = [(0, 0), (0, 1), (1, 0), (1, 1), (0, 2), (2, 0)]
N_CONST = 3
ROW_PART = N_STAIR
ROW_CONST = ROW_PART + len(PART_PAIRS) * HS
K_RAW = ROW_CONST + N_CONST
K_SUB = K_RAW + 3

NW, WT = T // WIN, WIN // P
MAX_UNITS = [[(3, 0, 2), (3, 2, 2), (2, 0, 2), (2, 2, 2), (1, 0, 4), (0, 0, 4)],
             [(i, h, 1) for i in (7, 6, 5, 4) for h in range(G)]]
EXP_UNITS, PV_STEPS = [[], []], [[], []]
for _w in range(NW):
    for _c in range(2 * _w + 2):
        _full = _c < 2 * _w + 1
        _t0, _n = (_w * WIN, WIN) if _full else (_c * 2 * P, 2 * P)
        for _h in ((0, 2) if _full else (0,)):
            EXP_UNITS[_w].append((_c, _h, 2 if _full else 4, _t0, _n))
        PV_STEPS[_w].append((_c, _t0, _n, len(EXP_UNITS[_w])))
NPT = 4


def numbering(units):
    return (lambda w, g, n: w * NG * len(units[0]) + g * len(units[w]) + n), NG * (len(units[0]) + len(units[1]))


pos_max, MAXN = numbering(MAX_UNITS)
pos_exp, EXPN = numbering(EXP_UNITS)
pos_pv, PVN = numbering(PV_STEPS)

POST_STEPS = ["norm", "aT", "proj", "stats", "apply", "xT", "logits", "score", "pairs", "groups", "experts",
              "weights", "parts", "cT"]
POST_SPACED = ["norm", None, "aT", "proj", "stats", "apply", None, "xT", "logits", "score", "pairs", "groups", "experts",
               "weights", "parts", None, "cT"]
UNITS = NW * NCH
LAG = 3
Y0_AT = NCH + LAG + 3
CHUNKS = [16, 17] + list(range(16))
POST_AT = {v: [step] for v, step in enumerate(POST_STEPS)}
PREP_AT = {14: ["ln_stats"], 16: ["ln_apply0"], 17: ["ln_apply1", "f0"], 18: ["f1"], 19: ["f4", "f5"], 20: ["tails_k", "f2"],
           21: ["sums_k", "f3"], 22: ["ksplit", "f6"], 23: ["qsplit0", "f7", "tails_v"], 24: ["qsplit1"], 25: ["prod", "sums_v"],
           26: ["f11"], 28: ["f8", "f9", "f10"]}
PREP_ALL = [st for u in sorted(PREP_AT) for st in PREP_AT[u]]
FILL_ORDER = [st for st in PREP_ALL if st[0] == "f"]
FILLS = len(FILL_ORDER)
fill_no = {st: n for n, st in enumerate(FILL_ORDER)}
LEAD_GROUPS = 2
LEAD = []
for _g in range(LEAD_GROUPS):
    LEAD += [("max", 0, _g, n) for n in range(len(MAX_UNITS[0]))] + [("mfin", 0, _g, 0)]
    if _g == 1:
        LEAD.insert(len(LEAD) - 4, ("mT", 0, 0, 0))
LEAD_FROM = 30
LEAD_AT = {}
for _n, _ev in enumerate(LEAD):
    LEAD_AT.setdefault(LEAD_FROM + _n * 10 // len(LEAD), []).append(_ev)
FFN_SLOTS = max(UNITS + LAG, max(LEAD_AT) + 1)


AHEAD, SPREAD, PV_LAG = 4, 0.8, 2
POST_COST = {"norm": 500, "aT": 0, "proj": 700, "stats": 900, "apply": 500, "xT": 0, "logits": 0, "score": 1100,
             "pairs": 1300, "groups": 1400, "experts": 1400, "weights": 800, "parts": 800, "cT": 0}


def attention_order():
    maxes = []
    for w in range(NW):
        for g in range(NG):
            if w == 0 and g < LEAD_GROUPS:
                continue
            for n, (i, h0, nh) in enumerate(MAX_UNITS[w]):
                maxes.append((BLK * (i + 1) * nh + 130, ("max", w, g, n)))
                if n == 4 and (w, g) != (0, 1):
                    maxes.append((100, ("mT",) + divmod(NG * w + g - 1, NG) + (0,)))
            maxes.append((450, ("mfin", w, g, 0)))
            if g == NG - 1:
                maxes.append((100, ("tail", w, 0, 0)))
    flat = [(w, g, n) for w in range(NW) for g in range(NG) for n in range(len(EXP_UNITS[w]))]
    steps = [(w, g, k) for w in range(NW) for g in range(NG) for k in range(len(PV_STEPS[w]))]
    post = list(POST_SPACED)
    total = sum(c for c, _ in maxes) + sum(POST_COST.values())
    order, seen, spent, done, post_from, last_max = [], {("mT", 0, 0)}, 0, 0, None, None
    late = {}
    for n in range(len(flat) + 7):
        other = [("exp",) + flat[n]] if n < len(flat) else []
        other += late.pop(n, [])
        while done < len(steps) and pos_exp(*steps[done][:2], PV_STEPS[steps[done][0]][steps[done][2]][3]) <= n - PV_LAG:
            w, g, k = steps[done]
            other.append(("pv", w, g, k))
            done += 1
            if k == len(PV_STEPS[w]) - 1:
                late.setdefault(n + 1, []).append(("oevac", w, g, 0))
                late.setdefault(n + 3, []).append(("oT", w, g, 0))
                if (w, g) == (0, NG - 1):
                    post_from = n + 4
        if post_from is not None and n >= post_from and post:
            step = post.pop(0)
            if step:
                spent += POST_COST[step]
                other.append(("post", 0, 0, step))
        if not maxes and last_max is None:
            last_max = n
        if last_max is not None and n == last_max + 1:
            other.append(("mT", NW - 1, NG - 1, 0))
        ahead = ("mT",) + flat[min(n + AHEAD, len(flat) - 1)][:2]
        mine = []
        while maxes and (spent < total * (n + 1.5) / (SPREAD * len(flat)) or ahead not in seen):
            cost, ev = maxes.pop(0)
            spent += cost
            seen.add(ev[:3])
            mine.append(ev)
        for k in range(max(len(other), len(mine))):
            order += other[k:k + 1] + mine[k:k + 1]
    assert not post and not maxes and done == len(steps)
    at = {}
    for k, ev in enumerate(order):
        at.setdefault(ev[:3], k)
    assert all(at["mT", w, g] < at["exp", w, g] for w in range(NW) for g in range(NG) if w or g)
    return order


ORDER = attention_order()


def misc_order():
    uses = [("mT", 0, 0), ("yT", 1, 0)]
    for kind, w, g, n in ORDER:
        if kind in ("mT", "oT"):
            uses.append((kind, w, g))
        if kind == "post" and n in ("aT", "proj", "xT", "logits", "cT"):
            uses.append((n, 0, 0))
    for v in range(UNITS):
        uses += [(st, 1, 0) for st in POST_AT.get(v, []) if st in ("aT", "proj", "xT", "logits", "cT")]
        if v == Y0_AT:
            uses.append(("yT", 0, 0))
    return {u: n for n, u in enumerate(uses)}


MISC = misc_order()
MISCN = len(MISC)


class Chain:

    def __init__(self, eng, sem, per, spare):
        self.eng, self.sem, self.per, self.spare = eng, sem, per, spare

    def begin(self, b):
        self.b, self.n = b, 0

    def __call__(self, ins):
        self.n += 1
        ins.then_inc(self.sem, 1)
        self.eng.wait_ge(self.sem, self.b * self.per + self.n)

    def alone(self, ins):
        self(ins)
        self.eng.sem_inc(self.spare, 1)

    def end(self):
        assert self.n == self.per, (self.n, self.per)


def build(nc, x, w_qkv, w_proj, gate, e_bias, up, down, ident_c, head_sel_c, q_stair_c, k_stair_c,
          q_rows_c, k_rows_c, exp_sel_c, out):
    f32, bf16, f32r = mybir.dt.float32, mybir.dt.bfloat16, mybir.dt.float32r
    ALU, ACT, AX = mybir.AluOpType, mybir.ActivationFunctionType, mybir.AxisListType
    ctx = ExitStack()
    with ctx:
        def sb(name, shape, dt=f32):
            return ctx.enter_context(nc.sbuf_tensor(name, shape, dt))

        def sem(name):
            return ctx.enter_context(nc.semaphore(name))

        wqkv = sb("wqkv", [P, 3 * C])
        wproj = sb("wproj", [P, C])
        wgate = sb("wgate", [P, NE])
        WGH, WGL = sb("WGH", [P, NE], f32r), sb("WGL", [P, NE], f32r)
        WUH, WUL = sb("WUH", [P, NCH * P], f32r), sb("WUL", [P, NCH * P], f32r)
        bias = sb("bias", [P, NE])
        wdown = sb("wdown", [P, NCH, C])
        ident = sb("ident", [P, P])
        identb = sb("identb", [P, P], bf16)
        head_sel = sb("head_sel", [P, NH])
        exp_sel = sb("exp_sel", [3 * NE, 16, P], bf16)
        X = sb("X", [P, NT, C])
        stats = sb("stats", [P, NT, 6])
        mv = sb("mv", [P, NT, 2])
        var = sb("var", [P, NT])
        neg_half = sb("neg_half", [P, NT])
        rstd = sb("rstd", [P, NT])
        XN = sb("XN", [P, NT, C])
        XNT = sb("XNT", [P, T])
        QT = sb("QT", [P, T])
        TAIL = sb("TAIL", [P, 2, T // 4, 4])
        SUMS = sb("SUMS", [P, 2, NT, BLK])
        Qparts = sb("Qparts", [P, 3, T], bf16)
        Kparts = sb("Kparts", [P, 3, NS], bf16)
        qrem = XN[:, :, :].rearrange("p i c -> p (i c)")
        krem = qrem[:, 0:NS]
        PROD = XNT
        QA = sb("QA", [K_SUB, NW, NH, WIN], bf16)
        KA = sb("KA", [K_SUB, NH, NS], bf16)
        VA = sb("VA", [P, NS // P, NH, 32])
        VTL = sb("VTL", [P, NT, C])
        TLG = sb("TLG", [P, NT, NH])
        MXR = sb("MXR", [P, NG, NT, G])
        MALL = sb("MALL", [P, NG, NW, G, WT])
        mrem = sb("mrem", [P, G * WT])
        MS = sb("MS", [P, 2, 3, G * WT], bf16)
        MB = sb("MB", [3 * G * WT, P], bf16)
        PT = sb("PT", [P, NPT, G, WIN])
        OS = sb("OS", [P, WIN])
        ATT = sb("ATT", [P, NT, NH, HS + 1])
        TD = sb("TD", [P, NT, NH])
        ET = sb("ET", [P, NT, NH])
        VW = sb("VW", [P, NT, C])
        DEN = sb("DEN", [P, NT, NH])
        AO = VW
        X1 = sb("X1", [P, NT, C])
        XH, XL = sb("XH", [P, T], f32r), sb("XL", [P, T], f32r)
        ATTT = XNT
        SCO = sb("SCO", [P, NT, NE])
        SCB = sb("SCB", [P, NT, NE])
        hi2 = sb("hi2", [P, 2, NT, NGRP, 2])
        grp = sb("grp", [P, NT, NGRP + 4])
        grpo = sb("grpo", [P, NT, NGRP + 4])
        top8 = sb("top8", [P, NT, 8])
        gmask = sb("gmask", [P, NT, NGRP])
        cand = sb("cand", [P, NT, NE + 2])
        cando = sb("cando", [P, NT, NE + 2])
        WSEL = sb("WSEL", [P, NT, NE])
        wsum = sb("wsum", [P, NT])
        wrem = sb("wrem", [P, NT, NE])
        CP = sb("CP", [P, NT, 3, NE], bf16)
        CT = sb("CT", [3 * NE, T], bf16)
        R, V, H = (PT[:, n, 0:4, :] for n in range(3))
        OT = PT[:, 3, 0:2, :]
        wup = PT[:, 0:2, :, :].rearrange("p a h t -> p (a h t)")[:, 0:NCH * P]
        Y = sb("Y", [P, 2, 4, C])

        st = ctx.enter_context(nc.psum_tensor("st", [P, 4, WIN], f32))
        mx = ctx.enter_context(nc.psum_tensor("mx", [P, 2, WIN], f32))
        om = ctx.enter_context(nc.psum_tensor("om", [P, 2, WIN], f32))
        misc, opsum = om[:, 0, :], om[:, 1, :]

        Qd = nc.dram_tensor("q_parts", [3, P, T], bf16, kind="Internal").ap()
        Kd = nc.dram_tensor("k_parts", [3, P, NS], bf16, kind="Internal").ap()

        s_w, s_w2 = sem("first_weights_loaded"), sem("other_weights_loaded")
        s_stair = sem("staircase_rows_loaded")
        s_x = sem("x_loaded")
        s_out = sem("out_stored")
        s_init = sem("constants_set")
        s_qd = [sem(f"q_parts_stored_{w}") for w in range(NW)]
        s_kd = sem("k_parts_stored")
        s_qa = [sem(f"qa_loaded_{w}") for w in range(NW)]
        s_ka = sem("ka_loaded")
        s_mrow = sem("max_rows_loaded")
        s_wsplit, s_xh = sem("weights_split"), sem("xn2_high_ready")
        s_mfill, s_mfree = sem("misc_filled"), sem("misc_free")
        s_var1, s_rstd1, s_xn1 = sem("var1_ready"), sem("rstd1_ready"), sem("xn1_ready")
        s_pfill, s_pevac = sem("prep_bank_filled"), sem("prep_bank_evacuated")
        s_tails, s_sums, s_prod = sem("tails_v_ready"), sem("sums_v_ready"), sem("prod_ready")
        s_qsplit, s_ksplit = sem("q_split"), sem("k_split")
        s_maxin, s_maxed = sem("max_unit_filled"), sem("max_unit_reduced")
        s_msplit, s_mb = sem("max_split"), sem("max_rows_ready")
        s_expin, s_exped = sem("exp_unit_filled"), sem("exp_unit_done")
        s_pv, s_oevac = sem("pv_done"), sem("o_evacuated")
        s_td, s_et = sem("tail_diff_ready"), sem("tail_exp_ready")
        s_tv, s_den = sem("tail_v_weighted"), sem("denominators_ready")
        s_ao = sem("attn_out_ready")
        s_x1 = sem("x1_ready")
        s_var2, s_rstd2, s_xn2 = sem("var2_ready"), sem("rstd2_ready"), sem("xn2_ready")
        s_cp = sem("combine_ready")
        s_up, s_bc, s_dn = sem("up_done"), sem("weights_broadcast"), sem("down_done")
        s_relu, s_vw, s_h = sem("relu_done"), sem("weighted"), sem("hidden_ready")
        s_dev, s_y = sem("down_evacuated"), sem("y_ready")
        s_spare = sem("spare")
        s_cd1, s_cd2, s_cd3 = sem("dve_chain_prep"), sem("dve_chain_post"), sem("dve_chain_maxima")
        s_cd4 = sem("dve_chain_norm")
        s_cp1, s_cp2 = sem("pool_chain_prep"), sem("pool_chain_norm")

        N_FIRST, N_OTHER = 6, 6
        done_after = lambda st_: fill_no[st_] + 1
        parity = lambda n: mx[:, n % 2, :]

        block = ctx.enter_context(nc.Block())

        def batches(eng, body):
            with eng.Fori(0, B - 1) as b:
                body(b, False)
            body(B - 1, True)

        def tails(eng, chain, a):
            add = lambda dst, x, y: chain(eng.tensor_tensor(dst, x, y, ALU.add))
            for j in (1, 2):
                add(TAIL[:, a, :, j], TAIL[:, a, :, j], TAIL[:, a, :, j - 1])
            add(SUMS[:, a, :, 0:32], *(TAIL[:, a, :, j].rearrange("p (i s) -> p i s", i=NT) for j in (2, 3)))
            add(TAIL[:, a, :, 3], TAIL[:, a, :, 3], TAIL[:, a, :, 2])

        def sums(eng, chain, a):
            add = lambda dst, x, y: chain(eng.tensor_tensor(dst, x, y, ALU.add))
            at, n, L = 0, 32, BLK - 1
            while n > 1:
                pair = SUMS[:, a, :, at:at + n].rearrange("p i (s two) -> p i s two", two=2)
                add(SUMS[:, a, :, at + n:at + n + n // 2], pair[:, :, :, 0], pair[:, :, :, 1])
                at, n = at + n, n // 2
            half = SUMS[:, a, :, :].rearrange("p (i two) s -> p i two s", two=2)
            add(half[:, :, 1, L], half[:, :, 0, L - 1], half[:, :, 1, L - 1])
            for i in (0, 4):
                add(SUMS[:, a, i + 2, L:L + 1], SUMS[:, a, i + 1, L:L + 1], SUMS[:, a, i + 3, L:L + 1])
            add(SUMS[:, a, 4, L:L + 1], SUMS[:, a, 2, L:L + 1], SUMS[:, a, 6, L:L + 1])

        def by_head(w):
            t = slice(WT * w, WT * w + WT)
            return (lambda a: a[:, t, :].rearrange("p i (h d) -> p (i h) d", d=HS),
                    lambda a: a[:, t, :].rearrange("p i h -> p (i h)").unsqueeze(2).to_broadcast([P, WT * NH, HS]))

        def sets_out(w):
            return ATT[:, WT * w:WT * w + WT, :, 0:HS].rearrange("p i h d -> p (i h) d")

        def filled(eng, b, use):
            eng.wait_ge(s_mfill, b * MISCN + MISC[use] + 1)

        def freed(eng, b, use):
            eng.wait_ge(s_mfree, b * MISCN + MISC[use] + 2)

        @block.sync
        def _(sp):
            def load_x(p, first):
                if not first:
                    sp.wait_ge(s_x1, NW * p)
                src = x[bass.ds(p, 1)].rearrange("o (i p) c -> p (o i) c", p=P)
                sp.dma_start(X[:, :, :], src).then_inc(s_x, 16)

            def prep(p):
                sp.wait_ge(s_ksplit, p + 1)
                sp.dma_start(Kd.rearrange("a p s -> p a s"), Kparts[:, :, :]).then_inc(s_kd, 16)

                def store_q(w):
                    sp.wait_ge(s_qsplit, NW * p + w + 1)
                    win = slice(WIN * w, WIN * w + WIN)
                    sp.dma_start(Qd[:, :, win].rearrange("a p s -> p a s"), Qparts[:, :, win]).then_inc(s_qd[w], 16)

                def load_q(w):
                    sp.wait_ge(s_qd[w], 16 * p + 16)
                    for n, (part, _) in enumerate(PART_PAIRS):
                        r = ROW_PART + n * HS
                        src = Qd[part].rearrange("(h d) s -> d h s", d=HS)[:, :, WIN * w:WIN * w + WIN]
                        sp.dma_start(QA[r:r + HS, w, :, :], src).then_inc(s_qa[w], 16)

                store_q(0)
                sp.wait_ge(s_kd, 16 * p + 16)
                for n, (_, part) in enumerate(PART_PAIRS):
                    r = ROW_PART + n * HS
                    sp.dma_start(KA[r:r + HS, :, :], Kd[part].rearrange("(h d) s -> d h s", d=HS)).then_inc(s_ka, 16)
                load_q(0)
                store_q(1)
                load_q(1)

            def store_y(b, w):
                sp.wait_ge(s_y, NW * b + w + 1)
                dst = out[bass.ds(b, 1), WIN * w:WIN * w + WIN].rearrange("o (i p) c -> p (o i) c", p=P)
                sp.dma_start(dst, Y[:, w, :, :]).then_inc(s_out, 16)

            sp.sem_inc(s_out, 1)
            load_x(0, True)
            for dst, src in ((wqkv, w_qkv), (ident, ident_c), (head_sel, head_sel_c)):
                sp.dma_start(dst[:, :], src).then_inc(s_w, 16)
            for w in range(NW):
                sp.dma_start(QA[ROW_CONST:K_RAW, w, :, :], q_rows_c[:, WIN * w:WIN * w + WIN].unsqueeze(1)
                             .to_broadcast([N_CONST, NH, WIN])).then_inc(s_w, 16)
            sp.dma_start(KA[ROW_CONST:K_SUB, :, :], k_rows_c.unsqueeze(1).to_broadcast([K_SUB - ROW_CONST, NH, NS])).then_inc(s_w, 16)
            sp.dma_start(KA[0:N_STAIR, :, :], k_stair_c.unsqueeze(1).to_broadcast([N_STAIR, NH, NS])).then_inc(s_stair, 16)
            sp.dma_start(QA[0:N_STAIR, :, :, :].rearrange("k w h t -> k (w h) t"),
                         q_stair_c.unsqueeze(1).to_broadcast([N_STAIR, NW * NH, WIN])).then_inc(s_stair, 16)
            for dst, src in ((wproj[:, :], w_proj), (wgate[:, :], gate), (wup, up)):
                sp.dma_start(dst, src).then_inc(s_w2, 16)
            sp.dma_start(bias[:, :], e_bias.partition_broadcast(P)).then_inc(s_w2, 16)
            sp.dma_start(wdown[:, :, :], down.rearrange("(k p) c -> p k c", p=P)).then_inc(s_w2, 16)
            sp.dma_start(exp_sel[:, :, :], exp_sel_c).then_inc(s_w2, 16)
            prep(0)

            def maxima_rows(b, n):
                w, g = n // NG, n % NG
                sp.wait_ge(s_mb, b * NW * NG + n + 1)
                sp.dma_start(QA[K_RAW:K_SUB, w, G * g:G * g + G, :].rearrange("a h t -> a (h t)"), MB[:, :]).then_inc(s_mrow, 16)
            maxima_rows(0, 0)

            def body(b, last):
                for n in range(1, NW * NG):
                    maxima_rows(b, n)
                if not last:
                    load_x(b + 1, False)
                    prep(b + 1)
                store_y(b, 0)
                if not last:
                    maxima_rows(b + 1, 0)
                store_y(b, 1)
            batches(sp, body)
            sp.wait_ge(s_out, NW * 16 * B + 1)
            sp.wait_ge(s_kd, 16 * B)
            for w in range(NW):
                sp.wait_ge(s_qd[w], 16 * B)

        @block.gpsimd
        def _(pool):
            pool.memset(neg_half[:, :], -0.5).then_inc(s_init, 1)
            pool.memset(VA[:, :, :, :], 0.0).then_inc(s_init, 1)
            pool.wait_ge(s_init, 2)
            pool.memset(VA[:, :, :, HS:HS + 1], 1.0).then_inc(s_init, 1)
            pool.memset(grp[:, :, 0:4], BIG).then_inc(s_init, 1)
            pool.memset(cand[:, :, 0:2], BIG).then_inc(s_init, 1)
            pool.memset(SUMS[:, :, 0, BLK - 1:BLK], 0.0).then_inc(s_init, 1)
            pool.wait_ge(s_w, 16 * N_FIRST)
            pool.tensor_copy(identb[:, :], ident[:, :]).then_inc(s_init, 1)

            chain1 = Chain(pool, s_cp1, 13, s_spare)
            chain2 = Chain(pool, s_cp2, 1, s_spare)

            def prep_step(p, step):
                if step == "ln_stats":
                    pool.wait_ge(s_var1, p + 1)
                    pool.tensor_tensor(rstd[:, :], var[:, :], neg_half[:, :], ALU.pow).then_inc(s_rstd1, 1)
                elif step == "tails_v":
                    chain1.begin(p)
                    pool.wait_ge(s_pevac, p * FILLS + max(done_after("f6"), done_after("f7")))
                    tails(pool, chain1, 1)
                    pool.sem_inc(s_tails, 1)
                elif step == "sums_v":
                    sums(pool, chain1, 1)
                    pool.sem_inc(s_sums, 1)
                    chain1.end()

            def tail_weights(b, w):
                pool.wait_ge(s_et, NW * b + w + 1)
                heads, flat = by_head(w)
                pool.tensor_tensor(heads(VW), heads(VTL), flat(ET), ALU.mult).then_inc(s_tv, 1)

            def post_step(b, w, step):
                if step == "norm" and w == 0:
                    heads, flat = by_head(w)
                    chain2.begin(b)
                    freed(pool, b, ("oT", w, NG - 1))
                    pool.wait_ge(s_tv, NW * b + w + 1)
                    chain2(pool.tensor_tensor(heads(VW), heads(VW), sets_out(w), ALU.add))
                    pool.wait_ge(s_den, b + 1)
                    pool.tensor_tensor(heads(AO), heads(VW), flat(DEN), ALU.mult).then_inc(s_ao, 1)
                elif step == "stats":
                    pool.wait_ge(s_var2, NW * b + w + 1)
                    pool.tensor_tensor(rstd[:, WT * w:WT * w + WT], var[:, WT * w:WT * w + WT], neg_half[:, 0:WT],
                                       ALU.pow).then_inc(s_rstd2, 1)

            def body(b, last):
                for kind, w, g, n in ORDER:
                    if kind == "tail":
                        tail_weights(b, w)
                    elif kind == "post":
                        post_step(b, w, n)
                for u in range(UNITS):
                    for step in POST_AT.get(u, []):
                        post_step(b, 1, step)
                    if not last:
                        for step in PREP_AT.get(u, []):
                            prep_step(b + 1, step)
                    routed = (u // NCH) * 16 + u % NCH - 2
                    if u >= 4:
                        pool.wait_ge(s_dn, b * UNITS + u - 3)
                    if CHUNKS[u % NCH] < 16:
                        pool.wait_ge(s_vw, b * 32 + routed + 1)
                        src = V
                    else:
                        pool.wait_ge(s_relu, b * UNITS + u + 1)
                        src = R
                    pool.tensor_tensor(H[:, u % 4, :], src[:, u % 4, :], R[:, u % 4, :], ALU.mult).then_inc(s_h, 1)

            for step in PREP_ALL:
                prep_step(0, step)
            batches(pool, body)

        @block.scalar
        def _(act):
            def prep_step(p, step):
                if step[0] != "f":
                    return
                n = fill_no[step]
                bank = parity(n)
                act.wait_ge(s_pfill, p * FILLS + n + 1)
                if step in ("f0", "f1"):
                    k = int(step[1])
                    ins = act.activation(XNT[:, WIN * k:WIN * k + WIN], bank, ACT.Copy)
                elif step in ("f2", "f3"):
                    k = int(step[1]) - 2
                    ins = act.activation(QT[:, WIN * k:WIN * k + WIN], bank, ACT.Copy)
                elif step in ("f4", "f5", "f6", "f7"):
                    k = int(step[1]) - 4
                    ins = act.activation(TAIL[:, k // 2, P * (k % 2):P * (k % 2) + P, :],
                                         bank.rearrange("p (n j) -> p n j", j=4), ACT.Copy)
                elif step == "f8":
                    ins = act.activation(VA[:, :, :, 0:HS], bank.rearrange("p (c h d) -> p c h d", c=4, d=HS), ACT.Copy)
                elif step in ("f9", "f10"):
                    k = int(step[1:]) - 9
                    ins = act.activation(VTL[:, 4 * k:4 * k + 4, :], bank.rearrange("p (i c) -> p i c", i=4), ACT.Copy)
                else:
                    ins = act.activation(TLG[:, :, :], bank[:, 0:P].rearrange("p (i h) -> p i h", i=NT), ACT.Copy)
                ins.then_inc(s_pevac, 1)

            def post_step(b, w, step):
                t0 = WIN * w
                if step not in ("aT", "xT", "logits", "cT"):
                    return
                filled(act, b, (step, w, 0))
                if step == "aT":
                    ins = act.activation(ATTT[:, t0:t0 + WIN], misc, ACT.Copy)
                elif step == "xT":
                    act.activation(XH[:, t0:t0 + WIN], misc, ACT.Copy).then_inc(s_xh, 1)
                    return
                elif step == "logits":
                    ins = act.activation(SCO[:, WT * w:WT * w + WT, :], misc[:, 0:WT * NE].rearrange("p (i e) -> p i e", i=WT),
                                         ACT.Exp, scale=-1.0)
                else:
                    ins = act.activation(CT[:, t0:t0 + WIN], misc.bitcast(bf16)[0:3 * NE, 0:WIN], ACT.Copy)
                ins.then_inc(s_mfree, 1)

            def attend(b):
                for kind, w, g, n in ORDER:
                    if kind == "exp":
                        c, h0, nh, t0, nt = EXP_UNITS[w][n]
                        u = pos_exp(w, g, n)
                        k = pos_pv(w, g, [x[0] for x in PV_STEPS[w]].index(c))
                        act.wait_ge(s_expin, b * EXPN + u + 1)
                        if k >= NPT:
                            act.wait_ge(s_pv, b * PVN + k - NPT + 1)
                        src = st[:, 2 * (u % 2):2 * (u % 2) + 2, :].rearrange("p k (h t) -> p (k h) t", t=nt)
                        act.activation(PT[:, k % NPT, h0:h0 + nh, 0:nt], src, ACT.Exp, scale=SCALE).then_inc(s_exped, 1)
                    elif kind == "oevac":
                        act.wait_ge(s_pv, b * PVN + pos_pv(w, g, len(PV_STEPS[w]) - 1) + 1)
                        if (w, g) != (0, 0):
                            filled(act, b, ("oT", w, g - 1) if g else ("oT", w - 1, NG - 1))
                        act.activation(OS[:, :], opsum, ACT.Copy).then_inc(s_oevac, 1)
                    elif kind == "tail":
                        act.wait_ge(s_td, NW * b + w + 1)
                        act.activation(ET[:, WT * w:WT * w + WT, :], TD[:, WT * w:WT * w + WT, :], ACT.Exp,
                                       scale=SCALE).then_inc(s_et, 1)
                    elif kind == "post":
                        post_step(b, w, n)

            def down_evac(b, w):
                act.wait_ge(s_dn, b * UNITS + NCH * (w + 1))
                if w == 0:
                    pass
                act.activation(OT[:, w, :], opsum, ACT.Copy).then_inc(s_dev, 1)

            def ffn(b, last):
                for u in range(UNITS):
                    for step in POST_AT.get(u, []):
                        post_step(b, 1, step)
                    if not last:
                        for step in PREP_AT.get(u, []):
                            prep_step(b + 1, step)
                    act.wait_ge(s_up, b * UNITS + u + 1)
                    if u >= 4:
                        act.wait_ge(s_h, b * UNITS + u - 3)
                    act.activation(R[:, u % 4, :], st[:, u % 2, :], ACT.Relu).then_inc(s_relu, 1)
                    if u == NCH + LAG - 1:
                        down_evac(b, 0)
                down_evac(b, 1)

            act.wait_ge(s_init, 6)
            for step in PREP_ALL:
                if step == "f11":
                    act.wait_ge(s_w2, 16 * N_OTHER)
                    act.activation(WUH[:, :], wup, ACT.Copy).then_inc(s_wsplit, 1)
                    act.activation(WGH[:, :], wgate[:, :], ACT.Copy).then_inc(s_wsplit, 1)
                prep_step(0, step)
            act.wait_ge(s_wsplit, 4)

            def body(b, last):
                attend(b)
                ffn(b, last)
            batches(act, body)

        @block.tensor
        def _(pe):
            def use_misc(b, use):
                pe.wait_ge(s_mfree, b * MISCN + MISC[use] + 1)

            def prep_step(p, step, first):
                if step[0] != "f":
                    return
                n = fill_no[step]
                bank = parity(n)
                if n >= 2:
                    pe.wait_ge(s_pevac, p * FILLS + n - 1)
                elif not first:
                    pe.wait_ge(s_maxed, p * MAXN)
                if step in ("f0", "f1"):
                    k = int(step[1])
                    pe.wait_ge(s_xn1, p * NT + WT * k + WT)
                    for i in range(WT):
                        ins = pe.transpose(bank[:, P * i:P * i + P], XN[:, WT * k + i, :], ident[:, :])
                elif step in ("f2", "f3", "f4", "f5", "f6", "f7"):
                    k = int(step[1]) - 2
                    pe.wait_ge(s_pevac, p * FILLS + done_after("f1"))
                    ins = pe.matmul(bank, wqkv[:, C * (k // 2):C * (k // 2) + C],
                                    XNT[:, WIN * (k % 2):WIN * (k % 2) + WIN], start=True, stop=True)
                elif step == "f8":
                    pe.wait_ge(s_sums, p + 1)
                    for c in range(4):
                        ins = pe.transpose(bank[:, P * c:P * c + P],
                                           SUMS[:, 1, 2 * c:2 * c + 2, :].rearrange("p a s -> p (a s)"), ident[:, :])
                elif step in ("f9", "f10"):
                    k = int(step[1:]) - 9
                    pe.wait_ge(s_tails, p + 1)
                    for i in range(4):
                        v = TAIL[:, 1, 32 * (4 * k + i):32 * (4 * k + i) + 32, :].rearrange("p n j -> p (n j)")
                        ins = pe.transpose(bank[:, P * i:P * i + P], v, ident[:, :])
                else:
                    pe.wait_ge(s_prod, p + 1)
                    for i in range(NT):
                        ins = pe.matmul(bank[:, NH * i:NH * i + NH], PROD[:, P * i:P * i + P], head_sel[:, :],
                                        start=True, stop=True)
                ins.then_inc(s_pfill, 1)

            def post_step(b, w, step):
                if step not in ("aT", "proj", "xT", "logits", "cT"):
                    return
                use_misc(b, (step, w, 0))
                if step == "aT":
                    pe.wait_ge(s_ao, NW * b + w + 1)
                    for i in range(WT):
                        ins = pe.transpose(misc[:, P * i:P * i + P], AO[:, WT * w + i, :], ident[:, :])
                elif step == "proj":
                    freed(pe, b, ("aT", w, 0))
                    for i in range(WT):
                        t0 = P * (WT * w + i)
                        ins = pe.matmul(misc[:, P * i:P * i + P], ATTT[:, t0:t0 + P], wproj[:, :], start=True, stop=True)
                elif step == "xT":
                    pe.wait_ge(s_xn2, b * NT + WT * w + WT)
                    for i in range(WT):
                        ins = pe.transpose(misc[:, P * i:P * i + P], XN[:, WT * w + i, :], ident[:, :])
                elif step == "logits":
                    freed(pe, b, ("xT", w, 0))
                    for i in range(WT):
                        t0 = P * (WT * w + i)
                        pairs = [(xa, wa) for xa in (XH, XL) for wa in (WGH, WGL)]
                        for n, (xa, wa) in enumerate(pairs):
                            ins = pe.matmul(misc[:, NE * i:NE * i + NE], xa[:, t0:t0 + P], wa[:, :],
                                            start=(n == 0), stop=(n == 3), skip_group_check=True)
                else:
                    pe.wait_ge(s_cp, NW * b + w + 1)
                    for i in range(WT):
                        ins = pe.transpose(misc.bitcast(bf16)[0:3 * NE, P * i:P * i + P],
                                           CP[:, WT * w + i, :, :].rearrange("p a e -> p (a e)"), identb[:, :])
                ins.then_inc(s_mfill, 1)

            def max_unit(b, w, g, n):
                i, h0, nh = MAX_UNITS[w][n]
                u = pos_max(w, g, n)
                if u >= 2:
                    pe.wait_ge(s_maxed, b * MAXN + u - 1)
                else:
                    pe.wait_ge(s_pevac, (b + 1) * FILLS)
                    pe.wait_ge(s_ka, (b + 1) * len(PART_PAIRS) * 16)
                    pe.wait_ge(s_qa[0], (b + 1) * len(PART_PAIRS) * 16)
                if u == pos_max(1, 0, 0):
                    pe.wait_ge(s_qa[1], (b + 1) * len(PART_PAIRS) * 16)
                ns = BLK * (i + 1)
                for k in range(nh):
                    h = G * g + h0 + k
                    for r0, s0, s1 in ((ROW_PART, 0, ns - BLK), (0, ns - BLK, ns))[i == 0:]:
                        ins = pe.matmul(mx[:, u % 2, ns * k + s0:ns * k + s1],
                                        QA[r0:K_RAW, w, h, P * (i % WT):P * (i % WT) + P], KA[r0:K_RAW, h, s0:s1],
                                        start=True, stop=True)
                ins.then_inc(s_maxin, 1)

            def maxima_transpose(b, w, g):
                use_misc(b, ("mT", w, g))
                pe.wait_ge(s_msplit, (b * NW + w) * NG + g + 1)
                pe.sem_inc(s_spare, 1)
                pe.transpose(misc.bitcast(bf16)[0:3 * G * WT, 0:P], MS[:, g % 2, :, :].rearrange("p a m -> p (a m)"),
                             identb[:, :]).then_inc(s_mfill, 1)

            def attend(b):
                for kind, w, g, n in ORDER:
                    if kind == "max":
                        max_unit(b, w, g, n)
                    elif kind == "mT":
                        maxima_transpose(b, w, g)
                    elif kind == "exp":
                        c, h0, nh, t0, nt = EXP_UNITS[w][n]
                        u = pos_exp(w, g, n)
                        if n == 0:
                            pe.wait_ge(s_mrow, ((b * NW + w) * NG + g + 1) * 16)
                        if u >= 2:
                            pe.wait_ge(s_exped, b * EXPN + u - 1)
                        for k in range(nh):
                            h = G * g + h0 + k
                            own = c // 2 == w
                            for r0, a0, a1 in ((0, t0, t0 + 2 * P), (ROW_PART, t0 + 2 * P, t0 + nt)) if own else ((ROW_PART, t0, t0 + nt),):
                                if a0 == a1:
                                    continue
                                at = k * nt + a0 - t0
                                ins = pe.matmul(st[:, 2 * (u % 2) + at // WIN, at % WIN:at % WIN + a1 - a0],
                                                KA[r0:K_SUB, h, P * c:P * c + P], QA[r0:K_SUB, w, h, a0 - WIN * w:a1 - WIN * w],
                                                start=True, stop=True)
                        ins.then_inc(s_expin, 1)
                    elif kind == "pv":
                        c, t0, nt, need = PV_STEPS[w][n]
                        k = pos_pv(w, g, n)
                        pe.wait_ge(s_exped, b * EXPN + pos_exp(w, g, need))
                        o = NG * w + g
                        if c == 0 and o:
                            pe.wait_ge(s_oevac, b * NW * NG + o)
                        elif c == 0:
                            pe.wait_ge(s_dev, NW * b + 1)
                        for h in range(G):
                            ins = pe.matmul(opsum[32 * h:32 * h + 32, t0 - WIN * w:t0 - WIN * w + nt],
                                            VA[:, c, G * g + h, :], PT[:, k % NPT, h, 0:nt],
                                            start=(c == 0), stop=(c == 2 * w + 1), skip_group_check=True)
                        ins.then_inc(s_pv, 1)
                    elif kind == "oT":
                        use_misc(b, ("oT", w, g))
                        pe.wait_ge(s_oevac, (b * NW + w) * NG + g + 1)
                        for i in range(WT):
                            ins = pe.transpose(misc[:, P * i:P * i + P], OS[:, P * i:P * i + P], ident[:, :])
                        ins.then_inc(s_mfill, 1)
                    elif kind == "post":
                        post_step(b, w, n)

            def y_transpose(b, w, last):
                if w and last:
                    pe.wait_ge(s_mfree, (b + 1) * MISCN + 1)
                else:
                    use_misc(b + w, ("yT", w, 0))
                pe.wait_ge(s_dev, NW * b + w + 2)
                for i in range(WT):
                    ins = pe.transpose(misc[:, P * i:P * i + P], OT[:, w, P * i:P * i + P], ident[:, :])
                ins.then_inc(s_mfill, 1)

            def ffn(b, last):
                routed = 0
                for v in range(FFN_SLOTS):
                    if v < UNITS:
                        for step in POST_AT.get(v, []):
                            post_step(b, 1, step)
                        if not last:
                            for step in PREP_AT.get(v, []):
                                prep_step(b + 1, step, False)
                        w, k = v // NCH, CHUNKS[v % NCH]
                        if v == 0:
                            pe.wait_ge(s_wsplit, 4)
                            freed(pe, b, ("xT", 0, 0))
                            pe.wait_ge(s_exped, (b + 1) * EXPN)
                        if v == NCH:
                            freed(pe, b, ("xT", 1, 0))
                        if v >= 2:
                            pe.wait_ge(s_relu, b * UNITS + v - 1)
                        for n, (wa, xa) in enumerate(((WUH, XH), (WUH, XL), (WUL, XH))):
                            ins = pe.matmul(st[:, v % 2, :], wa[:, P * k:P * k + P], xa[:, WIN * w:WIN * w + WIN],
                                            start=(n == 0), stop=(n == 2))
                        ins.then_inc(s_up, 1)
                        if k < 16:
                            if routed % 16 == 0:
                                freed(pe, b, ("cT", w, 0))
                            if routed >= 2:
                                pe.wait_ge(s_vw, b * 32 + routed - 1)
                            pe.matmul(st[:, 2 + routed % 2, :], exp_sel[:, k, :], CT[:, WIN * w:WIN * w + WIN],
                                      start=True, stop=True).then_inc(s_bc, 1)
                            routed += 1
                    if LAG <= v < UNITS + LAG:
                        d = v - LAG
                        w, n = d // NCH, d % NCH
                        if d == 0:
                            pe.wait_ge(s_oevac, (b + 1) * NW * NG)
                        if d == NCH:
                            pe.wait_ge(s_dev, NW * b + 2)
                        pe.wait_ge(s_h, b * UNITS + d + 1)
                        pe.matmul(opsum, wdown[:, CHUNKS[n], :], H[:, d % 4, :],
                                  start=(n == 0), stop=(n == NCH - 1)).then_inc(s_dn, 1)
                    if v == Y0_AT:
                        y_transpose(b, 0, last)
                    if not last:
                        for kind, w, g, n in LEAD_AT.get(v, []):
                            if kind == "max":
                                max_unit(b + 1, w, g, n)
                            elif kind == "mT":
                                maxima_transpose(b + 1, w, g)
                y_transpose(b, 1, last)

            pe.wait_ge(s_w, 16 * N_FIRST)
            pe.wait_ge(s_init, 7)
            for step in PREP_ALL:
                prep_step(0, step, True)
            pe.wait_ge(s_stair, 32)
            for kind, w, g, n in LEAD:
                if kind == "max":
                    max_unit(0, w, g, n)
                elif kind == "mT":
                    maxima_transpose(0, w, g)
            pe.sem_inc(s_mfill, 1)

            def body(b, last):
                attend(b)
                ffn(b, last)
            batches(pe, body)

        @block.vector
        def _(dve):
            chain1 = Chain(dve, s_cd1, 24, s_spare)
            chain2 = Chain(dve, s_cd2, 30, s_spare)
            chain4 = Chain(dve, s_cd4, 4, s_spare)
            chain3 = Chain(dve, s_cd3, 4, s_spare)

            def ln_stats(src, chain, tiles, s_var):
                for i in tiles:
                    ins = dve.bn_stats(stats[:, i, :], src[:, i, :])
                chain.alone(ins)
                for i in tiles:
                    ins = dve.bn_aggr(mv[:, i, :], stats[:, i, :])
                chain(ins)
                t = slice(tiles[0], tiles[-1] + 1)
                dve.tensor_scalar(var[:, t], mv[:, t, 1], 1e-5, None, ALU.add).then_inc(s_var, 1)

            def ln_apply(src, tiles, s_rstd, v, s_xn):
                dve.wait_ge(s_rstd, v)
                for i in tiles:
                    dve.tensor_scalar(XN[:, i, :], src[:, i, :], mv[:, i, 0:1], rstd[:, i:i + 1],
                                      ALU.subtract, ALU.mult).then_inc(s_xn, 1)

            def prep_step(p, step, first):
                if step == "ln_stats":
                    chain1.begin(p)
                    dve.wait_ge(s_x, 16 * p + 16)
                    ln_stats(X, chain1, range(NT), s_var1)
                elif step in ("ln_apply0", "ln_apply1"):
                    t0 = WT * int(step[-1])
                    ln_apply(X, range(t0, t0 + WT), s_rstd1, p + 1, s_xn1)
                elif step == "tails_k":
                    dve.wait_ge(s_pevac, p * FILLS + max(done_after("f4"), done_after("f5")))
                    tails(dve, chain1, 0)
                elif step == "sums_k":
                    sums(dve, chain1, 0)
                elif step == "ksplit":
                    if not first:
                        dve.wait_ge(s_kd, 16 * p)
                    K = SUMS[:, 0, :, :].rearrange("p i s -> p (i s)")
                    chain1(dve.tensor_copy(Kparts[:, 0, :], K))
                    chain1(dve.tensor_tensor(krem, K, Kparts[:, 0, :], ALU.subtract))
                    chain1(dve.tensor_copy(Kparts[:, 1, :], krem))
                    dve.tensor_tensor(Kparts[:, 2, :], krem, Kparts[:, 1, :], ALU.subtract).then_inc(s_ksplit, 1)
                elif step in ("qsplit0", "qsplit1"):
                    w = int(step[-1])
                    win = slice(WIN * w, WIN * w + WIN)
                    dve.wait_ge(s_pevac, p * FILLS + done_after(f"f{2 + w}"))
                    if not first:
                        dve.wait_ge(s_qd[w], 16 * p)
                    chain1(dve.tensor_copy(Qparts[:, 0, win], QT[:, win]))
                    chain1(dve.tensor_tensor(qrem[:, win], QT[:, win], Qparts[:, 0, win], ALU.subtract))
                    chain1(dve.tensor_copy(Qparts[:, 1, win], qrem[:, win]))
                    dve.tensor_tensor(Qparts[:, 2, win], qrem[:, win], Qparts[:, 1, win], ALU.subtract).then_inc(s_qsplit, 1)
                elif step == "prod":
                    dve.wait_ge(s_pevac, p * FILLS + max(done_after("f6"), done_after("f7")))
                    dve.tensor_tensor(PROD[:, :], QT[:, :], TAIL[:, 0, :, :].rearrange("p n j -> p (n j)"),
                                      ALU.mult).then_inc(s_prod, 1)
                    chain1.end()

            def max_event(b, kind, w, g, n):
                if kind == "max":
                    i, h0, nh = MAX_UNITS[w][n]
                    u = pos_max(w, g, n)
                    ns = BLK * (i + 1)
                    dve.wait_ge(s_maxin, b * MAXN + u + 1)
                    dve.reduce_max(MXR[:, g, i, h0:h0 + nh], mx[:, u % 2, 0:ns * nh].rearrange("p (h s) -> p h s", s=ns),
                                   AX.X).then_inc(s_maxed, 1)
                elif kind == "mT":
                    filled(dve, b, ("mT", w, g))
                    if (w, g) != (0, 0):
                        dve.wait_ge(s_mrow, ((b * NW + w) * NG + g) * 16)
                    dve.tensor_copy(MB[:, :], misc.bitcast(bf16)[0:3 * G * WT, 0:P]).then_inc(s_mb, 1)
                    dve.wait_ge(s_mb, (b * NW + w) * NG + g + 1)
                    dve.sem_inc(s_mfree, 1)
                elif kind == "mfin":
                    t = slice(WT * w, WT * w + WT)
                    chain3.begin((b * NW + w) * NG + g)
                    dve.wait_ge(s_maxed, b * MAXN + pos_max(w, g, len(MAX_UNITS[w]) - 1) + 1)
                    chain3(dve.tensor_tensor(MALL[:, g, w, :, :], MXR[:, g, t, :].rearrange("p i h -> p h i"),
                                             TLG[:, t, G * g:G * g + G].rearrange("p i h -> p h i"), ALU.max))
                    if NG * w + g >= 2:
                        filled(dve, b, ("mT",) + divmod(NG * w + g - 2, NG))
                    M = MALL[:, g, w, :, :].rearrange("p h i -> p (h i)")
                    chain3(dve.tensor_copy(MS[:, g % 2, 0, 0:G * WT], M))
                    chain3(dve.tensor_tensor(mrem[:, :], M, MS[:, g % 2, 0, 0:G * WT], ALU.subtract))
                    chain3(dve.tensor_copy(MS[:, g % 2, 1, 0:G * WT], mrem[:, :]))
                    chain3.end()
                    dve.tensor_tensor(MS[:, g % 2, 2, 0:G * WT], mrem[:, :], MS[:, g % 2, 1, 0:G * WT], ALU.subtract).then_inc(s_msplit, 1)

            def attend(b):
                for kind, w, g, n in ORDER:
                    if kind in ("max", "mfin", "mT"):
                        max_event(b, kind, w, g, n)
                    elif kind == "tail":
                        t = slice(WT * w, WT * w + WT)
                        dve.tensor_tensor(TD[:, t, :].rearrange("p i (g h) -> p i g h", g=NG),
                                          TLG[:, t, :].rearrange("p i (g h) -> p i g h", g=NG),
                                          MALL[:, :, w, :, :].rearrange("p g h i -> p i g h"), ALU.subtract).then_inc(s_td, 1)
                    elif kind == "oT":
                        filled(dve, b, ("oT", w, g))
                        dve.tensor_copy(ATT[:, WT * w:WT * w + WT, G * g:G * g + G, :],
                                        misc.rearrange("p (i h d) -> p i h d", i=WT, h=G)[:, :, :, 0:HS + 1]).then_inc(s_mfree, 1)
                    elif kind == "post":
                        post_step(b, w, n)

            def post_step(b, w, step):
                t = slice(WT * w, WT * w + WT)
                if step == "norm":
                    chain2.begin(NW * b + w)
                    if w == 0:
                        chain4.begin(b)
                    heads, flat = by_head(w)
                    dve.wait_ge(s_et, NW * b + w + 1)
                    freed(dve, b, ("oT", w, NG - 1))
                    chain4(dve.tensor_tensor(DEN[:, t, :], ATT[:, t, :, HS], ET[:, t, :], ALU.add))
                    ins = dve.reciprocal(DEN[:, t, :], DEN[:, t, :])
                    if w == 0:
                        ins.then_inc(s_den, 1)
                        return
                    chain4(ins)
                    dve.wait_ge(s_tv, NW * b + w + 1)
                    chain4(dve.tensor_tensor(heads(VW), heads(VW), sets_out(w), ALU.add))
                    dve.tensor_tensor(heads(AO), heads(VW), flat(DEN), ALU.mult).then_inc(s_ao, 1)
                elif step == "proj":
                    filled(dve, b, ("proj", w, 0))
                    chain2(dve.tensor_tensor(X1[:, t, :], misc.rearrange("p (i c) -> p i c", i=WT), X[:, t, :], ALU.add))
                    dve.sem_inc(s_mfree, 1)
                    dve.sem_inc(s_x1, 1)
                elif step == "stats":
                    ln_stats(X1, chain2, range(WT * w, WT * w + WT), s_var2)
                elif step == "xT":
                    dve.wait_ge(s_xh, NW * b + w + 1)
                    win = slice(WIN * w, WIN * w + WIN)
                    dve.tensor_tensor(XL[:, win], misc, XH[:, win].bitcast(f32), ALU.subtract).then_inc(s_mfree, 1)
                elif step == "apply":
                    ln_apply(X1, range(WT * w, WT * w + WT), s_rstd2, NW * b + w + 1, s_xn2)
                elif step == "score":
                    freed(dve, b, ("logits", w, 0))
                    chain2(dve.tensor_scalar(SCO[:, t, :], SCO[:, t, :], 1.0, None, ALU.add))
                    chain2(dve.reciprocal(SCO[:, t, :], SCO[:, t, :]))
                    chain2(dve.tensor_tensor(SCB[:, t, :], SCO[:, t, :], bias[:, :].unsqueeze(1).to_broadcast([P, WT, NE]), ALU.add))
                elif step == "pairs":
                    four = SCB[:, t, :].rearrange("p i (g two k) -> p (i g) two k", g=NGRP, two=2)
                    hv, lv = hi2[:, 0, t, :, :], hi2[:, 1, t, :, :]
                    for v, op in ((hv, ALU.max), (lv, ALU.min)):
                        chain2(dve.tensor_tensor(v.rearrange("p i g k -> p (i g) k"), four[:, :, 0, :], four[:, :, 1, :], op))
                    first, second, third = (wrem[:, t, NGRP * k:NGRP * k + NGRP] for k in range(3))
                    chain2(dve.tensor_tensor(first, hv[:, :, :, 0], hv[:, :, :, 1], ALU.max))
                    chain2(dve.tensor_tensor(second, hv[:, :, :, 0], hv[:, :, :, 1], ALU.min))
                    chain2(dve.tensor_tensor(third, lv[:, :, :, 0], lv[:, :, :, 1], ALU.max))
                    chain2(dve.tensor_tensor(second, second, third, ALU.max))
                    chain2.alone(dve.tensor_tensor(grp[:, t, 4:], first, second, ALU.add))
                elif step == "groups":
                    choose(w, grp, grpo)
                    chain2(dve.tensor_tensor(gmask[:, t, :], grpo[:, t, 4:], grp[:, t, 4:], ALU.not_equal))
                    chain2(dve.tensor_tensor(WSEL[:, t, :].rearrange("p i (g k) -> p (i g) k", k=GE),
                                             SCB[:, t, :].rearrange("p i (g k) -> p (i g) k", k=GE),
                                             gmask[:, t, :].rearrange("p i g -> p (i g)").unsqueeze(2).to_broadcast([P, WT * NGRP, GE]), ALU.mult))
                    chain2.alone(dve.tensor_scalar(cand[:, t, 2:], WSEL[:, t, :], 0.0, None, ALU.add))
                elif step == "experts":
                    choose(w, cand, cando)
                    chain2(dve.tensor_tensor(WSEL[:, t, :], cando[:, t, 2:], cand[:, t, 2:], ALU.not_equal))
                    chain2(dve.tensor_tensor(WSEL[:, t, :], WSEL[:, t, :], SCO[:, t, :], ALU.mult))
                    chain2(dve.reduce_sum(wsum[:, t], WSEL[:, t, :], AX.X))
                elif step == "weights":
                    chain2(dve.tensor_scalar(wsum[:, t], wsum[:, t], 1e-20, None, ALU.add))
                    chain2(dve.reciprocal(wsum[:, t], wsum[:, t]))
                    chain2(dve.tensor_tensor(WSEL[:, t, :], WSEL[:, t, :], wsum[:, t].unsqueeze(2).to_broadcast([P, WT, NE]), ALU.mult))
                    chain2(dve.tensor_scalar(WSEL[:, t, :], WSEL[:, t, :], ROUTED_SCALE, None, ALU.mult))
                elif step == "parts":
                    chain2(dve.tensor_copy(CP[:, t, 0, :], WSEL[:, t, :]))
                    chain2(dve.tensor_tensor(wrem[:, t, :], WSEL[:, t, :], CP[:, t, 0, :], ALU.subtract))
                    chain2(dve.tensor_copy(CP[:, t, 1, :], wrem[:, t, :]))
                    chain2.end()
                    dve.tensor_tensor(CP[:, t, 2, :], wrem[:, t, :], CP[:, t, 1, :], ALU.subtract).then_inc(s_cp, 1)

            def choose(w, values, replaced):
                for i in range(WT * w, WT * w + WT):
                    ins = dve.max(top8[:, i, :], values[:, i, :])
                chain2.alone(ins)
                for i in range(WT * w, WT * w + WT):
                    ins = dve.match_replace(replaced[:, i, :], top8[:, i, :], values[:, i, :], -3.0 * BIG)
                chain2(ins)

            def finish(b, w, last):
                if w and last:
                    dve.wait_ge(s_mfill, (b + 1) * MISCN + 1)
                else:
                    filled(dve, b + w, ("yT", w, 0))
                dve.wait_ge(s_out, NW * 16 * b + 1)
                dve.tensor_tensor(Y[:, w, :, :], misc.rearrange("p (i c) -> p i c", i=WT),
                                  X1[:, WT * w:WT * w + WT, :], ALU.add).then_inc(s_y, 1)
                dve.wait_ge(s_y, NW * b + w + 1)
                dve.sem_inc(s_mfree, 1)

            def ffn(b, last):
                routed = 0
                for v in range(FFN_SLOTS):
                    if v < UNITS:
                        for step in POST_AT.get(v, []):
                            post_step(b, 1, step)
                        if not last:
                            for step in PREP_AT.get(v, []):
                                prep_step(b + 1, step, False)
                    u = v - 1
                    if 0 <= u < UNITS and CHUNKS[u % NCH] < 16:
                        dve.wait_ge(s_relu, b * UNITS + u + 1)
                        dve.wait_ge(s_bc, b * 32 + routed + 1)
                        if u >= 4:
                            dve.wait_ge(s_h, b * UNITS + u - 3)
                        dve.tensor_tensor(V[:, u % 4, :], R[:, u % 4, :], st[:, 2 + routed % 2, :], ALU.mult).then_inc(s_vw, 1)
                        routed += 1
                    if v == Y0_AT + 1:
                        finish(b, 0, last)
                    if not last:
                        for ev in LEAD_AT.get(v, []):
                            max_event(b + 1, *ev)
                finish(b, 1, last)

            dve.sem_inc(s_mfree, 1)
            dve.sem_inc(s_dev, 1)
            dve.wait_ge(s_init, 6)
            for step in PREP_ALL:
                prep_step(0, step, True)
            dve.wait_ge(s_wsplit, 2)
            for hi, lo, full in ((WUH, WUL, wup), (WGH, WGL, wgate[:, :])):
                dve.tensor_tensor(lo[:, :], full, hi[:, :].bitcast(f32), ALU.subtract).then_inc(s_wsplit, 1)
            for ev in LEAD:
                max_event(0, *ev)
            dve.sem_inc(s_mfree, 1)
            dve.wait_ge(s_w2, 16 * N_OTHER)

            def body(b, last):
                attend(b)
                ffn(b, last)
            batches(dve, body)


_INS = ["x", "w_qkv", "w_proj", "gate", "e_bias", "up", "down", "ident", "head_sel", "q_stair", "k_stair",
        "q_rows", "k_rows", "exp_sel"]


def layout(i):
    import numpy as np
    from concourse import mybir
    b16 = mybir.dt.np(mybir.dt.bfloat16)
    d = {k: np.asarray(v) for k, v in i.items()}
    up = np.concatenate([d["L0_ffn_up_w"].reshape(NE * 64, C), d["L0_ffn_shared_up_w"]], 0)
    down = np.concatenate([d["L0_ffn_down_w"].transpose(0, 2, 1).reshape(NE * 64, C), d["L0_ffn_shared_down_w"].T], 0)
    last = []
    n, size = 32, 4
    while n >= 1:
        last += [size * (k + 1) - 1 for k in range(n)]
        n, size = n // 2, size * 2
    last = np.array(last + [P - 1])
    t = np.arange(WIN) % (2 * P)
    q_stair = np.where(t[None, :] < 4 * np.arange(N_STAIR)[:, None] + 3, -BIG, 0.0)
    k_stair = np.zeros((N_STAIR, NT // 2, 2, BLK), np.float32)
    for odd in range(2):
        for slot in range(BLK - 1 + odd):
            k_stair[(last[slot] + P * odd) // 4, :, odd, slot] = 1.0
    k_stair = k_stair.reshape(N_STAIR, NS)
    tt = np.arange(T)
    q_rows = np.stack([tt >= 0, tt < 511, tt < 1023]).astype(np.float32)
    k_rows = np.zeros((K_SUB - ROW_CONST, NS), np.float32)
    k_rows[0, BLK - 1] = -BIG
    k_rows[1, 2 * BLK + BLK - 1] = -BIG
    k_rows[2, [4 * BLK + BLK - 1, 6 * BLK + BLK - 1]] = -BIG
    k_rows[3:] = -1.0
    head_sel = np.repeat(np.eye(NH, dtype=np.float32), HS, 0)
    exp_sel = np.zeros((3, NE, 16, P), np.float32)
    for e in range(NE):
        exp_sel[:, e, e // 2, 64 * (e % 2):64 * (e % 2) + 64] = 1.0
    return {
        "x": d["L0_attn_x"], "w_qkv": d["L0_attn_W_attn"].T, "w_proj": d["L0_attn_W_proj"].T,
        "gate": d["L0_ffn_gate_w"].T, "e_bias": d["L0_ffn_e_bias"], "up": up.T, "down": down,
        "ident": np.eye(P, dtype=np.float32), "head_sel": head_sel, 
        "q_stair": q_stair.astype(b16), "k_stair": k_stair.astype(b16), "q_rows": q_rows.astype(b16), "k_rows": k_rows.astype(b16),
        "exp_sel": exp_sel.reshape(3 * NE, 16, P).astype(b16),
    }


def kernel(**inputs):
    import numpy as _np
    import concourse.bacc as _bacc
    from concourse import mybir as _mybir
    from concourse.bass_utils import run_bass_kernel_spmd as _run

    nc = _bacc.Bacc("TRN2", target_bir_lowering=False, num_devices=1)
    laid = layout(inputs)
    arrays, args = {}, []
    for name in _INS:
        a = _np.ascontiguousarray(laid[name])
        arrays[f"in_{name}_dram"] = a
        args.append(nc.dram_tensor(f"in_{name}_dram", a.shape, _mybir.dt.from_np(a.dtype), kind="ExternalInput").ap())
    args.append(nc.dram_tensor("out_0_dram", (B, T, C), _mybir.dt.float32, kind="ExternalOutput").ap())
    build(nc, *args)
    r = _run(nc, [arrays], core_ids=[0])
    return r.results[0]["out_0_dram"]
```

```python
import concourse.bass as bass
from concourse import mybir
from contextlib import ExitStack

B, T, C = 4, 1024, 128
P = 128
NT = T // P
NH, HS = 16, 8
G, NG = 4, 4
NE, TOPK, NGRP, TOPG = 32, 6, 8, 4
GE = NE // NGRP
ROUTED_SCALE = 2.5
NCH = (NE * 64 + 256) // P
SCALE = 1.0 / float(HS) ** 0.5
BIG = 1e30
BLK = 64
NS = NT * BLK
WIN = 512

N_STAIR = 2 * (P // 4)
PART_PAIRS = [(0, 0), (0, 1), (1, 0), (1, 1), (0, 2), (2, 0)]
N_CONST = 3
ROW_PART = N_STAIR
ROW_CONST = ROW_PART + len(PART_PAIRS) * HS
K_RAW = ROW_CONST + N_CONST
K_SUB = K_RAW + 3

NW, WT = T // WIN, WIN // P
MAX_UNITS = [[(3, 0, 2), (3, 2, 2), (2, 0, 2), (2, 2, 2), (1, 0, 4), (0, 0, 4)],
             [(i, h, 1) for i in (7, 6, 5, 4) for h in range(G)]]
EXP_UNITS, PV_STEPS = [[], []], [[], []]
for _w in range(NW):
    for _c in range(2 * _w + 2):
        _full = _c < 2 * _w + 1
        _t0, _n = (_w * WIN, WIN) if _full else (_c * 2 * P, 2 * P)
        for _h in ((0, 2) if _full else (0,)):
            EXP_UNITS[_w].append((_c, _h, 2 if _full else 4, _t0, _n))
        PV_STEPS[_w].append((_c, _t0, _n, len(EXP_UNITS[_w])))
NPT = 4


def numbering(units):
    return (lambda w, g, n: w * NG * len(units[0]) + g * len(units[w]) + n), NG * (len(units[0]) + len(units[1]))


pos_max, MAXN = numbering(MAX_UNITS)
pos_exp, EXPN = numbering(EXP_UNITS)
pos_pv, PVN = numbering(PV_STEPS)

POST_STEPS = ["norm", "aT", "proj", "stats", "apply", "xT", "logits", "score", "pairs", "groups", "experts",
              "weights", "parts", "cT"]
UNITS = NW * NCH
LAG = 3
Y0_AT = NCH + LAG + 3
CHUNKS = [16, 17] + list(range(16))
POST_AT = {v: [step] for v, step in zip((0, 2, 3, 4, 5, 7, 8, 9, 10, 11, 12, 13, 14, 16), POST_STEPS)}
PREP_AT = {15: ["ln_stats"], 17: ["ln_apply0"], 18: ["ln_apply1"], 19: ["f0", "f1"], 20: ["f4", "f5"], 21: ["tails_k", "f2"],
           22: ["sums_k", "f3", "f6"], 23: ["ksplit", "f7"], 24: ["qsplit0", "tails_v"], 25: ["qsplit1"], 26: ["prod", "sums_v"],
           27: ["f11"], 29: ["f8", "f9", "f10"]}
PREP_ALL = [st for u in sorted(PREP_AT) for st in PREP_AT[u]]
FILL_ORDER = [st for st in PREP_ALL if st[0] == "f"]
FILLS = len(FILL_ORDER)
fill_no = {st: n for n, st in enumerate(FILL_ORDER)}
LEAD_GROUPS = 2
LEAD = []
for _g in range(LEAD_GROUPS):
    LEAD += [("max", 0, _g, n) for n in range(len(MAX_UNITS[0]))] + [("mfin", 0, _g, 0)]
    if _g == 1:
        LEAD.insert(len(LEAD) - 4, ("mT", 0, 0, 0))
LEAD_FROM = 30
LEAD_AT = {}
for _n, _ev in enumerate(LEAD):
    LEAD_AT.setdefault(LEAD_FROM + _n * 10 // len(LEAD), []).append(_ev)
FFN_SLOTS = max(UNITS + LAG, max(LEAD_AT) + 1)

POST_TIME = {"norm": (0, 3.4, 0.4), "aT": (0.9, 0.6, 0), "proj": (1.3, 0.8, 0.8), "stats": (0, 2.8, 1.6), "apply": (0, 1.1, 1.1),
             "xT": (0.9, 1.3, 0.7), "logits": (0.4, 0.3, 0), "score": (0, 1.2, 1.2), "pairs": (0, 1.3, 1.3),
             "groups": (0, 1.7, 1.7), "experts": (0, 1.7, 1.7), "weights": (0, 0.5, 0.5), "parts": (0, 2.5, 0), "cT": (0.3, 0.6, 0)}
MISC_STEPS = ("aT", "proj", "xT", "logits", "cT")
EAGER = 0.0
POST_GAP = 1.2


def attention_order():
    order, done = [], {}
    col = 0.45e-3
    free = {"pe": 0.0, "dve": 0.0, "act": 0.0, "misc": 0.0}
    maxes = [(w, g, n) for w in range(NW) for g in range(NG) if w or g >= LEAD_GROUPS for n in range(len(MAX_UNITS[w]))]
    exps = [(w, g, n) for w in range(NW) for g in range(NG) for n in range(len(EXP_UNITS[w]))]
    steps = [(w, g, k) for w in range(NW) for g in range(NG) for k in range(len(PV_STEPS[w]))]
    rows = [(w, g) for w in range(NW) for g in range(NG)][1:]
    turns, post, halves = [], list(POST_STEPS), []
    for g in range(LEAD_GROUPS):
        done["mfin", 0, g] = 0.0
    done["rows", 0, 0] = 0.0
    ring = lambda kind, u: done.get((kind, u - 2), 0.0)
    last_post = 0.0

    def run(ev, start, pe, eng, t):
        order.append(ev)
        free["pe"] = start + pe
        if not eng:
            return free["pe"]
        free[eng] = max(free[eng], free["pe"] + 0.3) + t
        return free[eng]

    while maxes or exps or steps or rows or turns or post:
        now, found = free["pe"], []
        if rows and ("mfin",) + rows[0] in done:
            found.append((max(now, done[("mfin",) + rows[0]] + 0.3, free["misc"]), 0, "mT"))
        if turns:
            found.append((max(now, done[("oevac",) + turns[0]] + 0.2, free["misc"]), 1, "oT"))
        if maxes:
            u = pos_max(*maxes[0])
            found.append((max(now, ring("max", u) + 0.1 - EAGER), 3, "max"))
        if halves:
            found.append((now, 4, halves[0]))
        if steps and "pv" not in halves:
            w, g, k = steps[0]
            need = ("exp", pos_exp(w, g, PV_STEPS[w][k][3]) - 1)
            if need in done:
                before = done.get(("oevac",) + divmod(NG * w + g - 1, NG), 0.0) if k == 0 else 0.0
                found.append((max(now, done[need] + 0.1, before + 0.1), 4 + bool(halves), "pv1"))
        if exps and "exp" not in halves:
            w, g, n = exps[0]
            u = pos_exp(w, g, n)
            k = pos_pv(w, g, [x[0] for x in PV_STEPS[w]].index(EXP_UNITS[w][n][0]))
            if ("rows", w, g) in done and (k < NPT or ("pv", k - NPT) in done):
                tile = done["pv", k - NPT] if k >= NPT else 0.0
                found.append((max(now, done["rows", w, g], ring("exp", u) + 0.1, tile), 6, "exp1"))
        if post and (0, NG - 1) not in turns and ("oT", 0, NG - 1) in done:
            step = post[0]
            ready = done["post"] if "post" in done else done["oT", 0, NG - 1]
            at = max(now, ready + 0.1, last_post + POST_GAP, free["misc"] if step in MISC_STEPS else 0.0)
            found.append((at, 2, "post"))
        start, _, kind = min(found)
        if kind == "mT":
            w, g = rows.pop(0)
            free["misc"] = run(("mT", w, g, 0), start, 0.15, "dve", 0.2)
            done["rows", w, g] = free["misc"] + 3.2
        elif kind == "oT":
            w, g = turns.pop(0)
            free["misc"] = done["oT", w, g] = run(("oT", w, g, 0), start, 0.6, "dve", 0.3)
        elif kind == "max":
            w, g, n = maxes.pop(0)
            i, _, nh = MAX_UNITS[w][n]
            cols = BLK * (i + 1) * nh
            done["max", pos_max(w, g, n)] = run(("max", w, g, n), start, cols * col + 0.06 * nh, "dve", 0.06 + cols * 1.05e-3)
            if n == len(MAX_UNITS[w]) - 1:
                order.append(("mfin", w, g, 0))
                free["dve"] += 0.15
                done["mfin", w, g] = free["dve"] + 1.2
                if g == NG - 1:
                    order.append(("tail", w, 0, 0))
        elif kind == "pv1":
            w, g, k = steps[0]
            halves.append("pv")
            run(("pv1", w, g, k), start, PV_STEPS[w][k][2] * 2 * 0.47e-3, None, 0)
        elif kind == "exp1":
            halves.append("exp")
            run(("exp1",) + exps[0], start, 512 * col + 0.08, None, 0)
        elif kind == "pv":
            halves.remove("pv")
            w, g, k = steps.pop(0)
            done["pv", pos_pv(w, g, k)] = run(("pv", w, g, k), start, PV_STEPS[w][k][2] * 2 * 0.47e-3, None, 0)
            if k == len(PV_STEPS[w]) - 1:
                order.append(("oevac", w, g, 0))
                free["act"] = max(free["act"], free["pe"] + 0.1) + 0.5
                done["oevac", w, g] = free["act"]
                turns.append((w, g))
        elif kind == "exp":
            halves.remove("exp")
            w, g, n = exps.pop(0)
            _, _, nh, _, nt = EXP_UNITS[w][n]
            done["exp", pos_exp(w, g, n)] = run(("exp", w, g, n), start, 512 * col + 0.08, "act", 0.9)
        else:
            step = post.pop(0)
            pe, rest, dve = POST_TIME[step]
            order.append(("post", 0, 0, step))
            last_post = start
            if pe:
                free["pe"] = start + pe
                start = free["pe"]
            if dve:
                free["dve"] = max(free["dve"], start) + dve
                done["post"] = free["dve"] + rest - dve
            else:
                done["post"] = start + rest
            if step in MISC_STEPS:
                free["misc"] = done["post"]
    return order


ORDER = attention_order()


def misc_order():
    uses = [("mT", 0, 0), ("yT", 1, 0)]
    for kind, w, g, n in ORDER:
        if kind in ("mT", "oT"):
            uses.append((kind, w, g))
        if kind == "post" and n in ("aT", "proj", "xT", "logits", "cT"):
            uses.append((n, 0, 0))
    for v in range(UNITS):
        uses += [(st, 1, 0) for st in POST_AT.get(v, []) if st in ("aT", "proj", "xT", "logits", "cT")]
        if v == Y0_AT:
            uses.append(("yT", 0, 0))
    return {u: n for n, u in enumerate(uses)}


MISC = misc_order()
MISCN = len(MISC)


class Chain:

    def __init__(self, eng, sem, per, spare):
        self.eng, self.sem, self.per, self.spare = eng, sem, per, spare

    def begin(self, b):
        self.b, self.n = b, 0

    def __call__(self, ins):
        self.n += 1
        ins.then_inc(self.sem, 1)
        self.eng.wait_ge(self.sem, self.b * self.per + self.n)

    def alone(self, ins):
        self(ins)
        self.eng.sem_inc(self.spare, 1)

    def end(self):
        assert self.n == self.per, (self.n, self.per)


def build(nc, x, w_qkv, w_proj, gate, e_bias, up, down, ident_c, head_sel_c, q_stair_c, k_stair_c,
          q_rows_c, k_rows_c, exp_sel_c, out):
    f32, bf16, f32r = mybir.dt.float32, mybir.dt.bfloat16, mybir.dt.float32r
    ALU, ACT, AX = mybir.AluOpType, mybir.ActivationFunctionType, mybir.AxisListType
    ctx = ExitStack()
    with ctx:
        def sb(name, shape, dt=f32):
            return ctx.enter_context(nc.sbuf_tensor(name, shape, dt))

        def sem(name):
            return ctx.enter_context(nc.semaphore(name))

        wqkv = sb("wqkv", [P, 3 * C])
        wproj = sb("wproj", [P, C])
        wgate = sb("wgate", [P, NE])
        WGH, WGL = sb("WGH", [P, NE], f32r), sb("WGL", [P, NE], f32r)
        WUH, WUL = sb("WUH", [P, NCH * P], f32r), sb("WUL", [P, NCH * P], f32r)
        bias = sb("bias", [P, NE])
        wdown = sb("wdown", [P, NCH, C])
        ident = sb("ident", [P, P])
        identb = sb("identb", [P, P], bf16)
        head_sel = sb("head_sel", [P, NH])
        exp_sel = sb("exp_sel", [3 * NE, 16, P], bf16)
        X = sb("X", [P, NT, C])
        stats = sb("stats", [P, NT, 6])
        mv = sb("mv", [P, NT, 2])
        var = sb("var", [P, NT])
        neg_half = sb("neg_half", [P, NT])
        zeros = sb("zeros", [P, WT * NE])
        rstd = sb("rstd", [P, NT])
        XN = sb("XN", [P, NT, C])
        XNT = sb("XNT", [P, T])
        QT = sb("QT", [P, T])
        TAIL = sb("TAIL", [P, 2, T // 4, 4])
        SUMS = sb("SUMS", [P, 2, NT, BLK])
        Qparts = sb("Qparts", [P, 3, T], bf16)
        Kparts = sb("Kparts", [P, 3, NS], bf16)
        qrem = XN[:, :, :].rearrange("p i c -> p (i c)")
        krem = qrem[:, 0:NS]
        PROD = XNT
        QA = sb("QA", [K_SUB, NW, NH, WIN], bf16)
        KA = sb("KA", [K_SUB, NH, NS], bf16)
        VA = sb("VA", [P, NS // P, NH, 32])
        VTL = sb("VTL", [P, NT, C])
        TLG = sb("TLG", [P, NT, NH])
        MXR = sb("MXR", [P, NG, NT, G])
        MALL = sb("MALL", [P, NG, NW, G, WT])
        mrem = sb("mrem", [P, G * WT])
        MS = sb("MS", [P, 2, 3, G * WT], bf16)
        MB = sb("MB", [3 * G * WT, P], bf16)
        PT = sb("PT", [P, NPT, G, WIN])
        OS = sb("OS", [P, WIN])
        ATT = sb("ATT", [P, NT, NH, HS + 1])
        TD = sb("TD", [P, NT, NH])
        ET = sb("ET", [P, NT, NH])
        VW = sb("VW", [P, NT, C])
        DEN = sb("DEN", [P, NT, NH])
        AO = VW
        X1 = sb("X1", [P, NT, C])
        XH, XL = sb("XH", [P, T], f32r), sb("XL", [P, T], f32r)
        ATTT = XNT
        SCO = sb("SCO", [P, NT, NE])
        SCB = sb("SCB", [P, NT, NE])
        hi2 = sb("hi2", [P, 2, NT, NGRP, 2])
        grp = sb("grp", [P, NT, NGRP + 4])
        grpo = sb("grpo", [P, NT, NGRP + 4])
        top8 = sb("top8", [P, NT, 8])
        gmask = sb("gmask", [P, NT, NGRP])
        cand = sb("cand", [P, NT, NE + 2])
        cando = sb("cando", [P, NT, NE + 2])
        WSEL = sb("WSEL", [P, NT, NE])
        wsum = sb("wsum", [P, NT])
        wrem = sb("wrem", [P, NT, NE])
        CP = sb("CP", [P, NT, 3, NE], bf16)
        CT = sb("CT", [3 * NE, T], bf16)
        R, V, H = (PT[:, n, 0:4, :] for n in range(3))
        OT = PT[:, 3, 0:2, :]
        wup = PT[:, 0:2, :, :].rearrange("p a h t -> p (a h t)")[:, 0:NCH * P]
        Y = sb("Y", [P, 2, 4, C])

        st = ctx.enter_context(nc.psum_tensor("st", [P, 4, WIN], f32))
        mx = ctx.enter_context(nc.psum_tensor("mx", [P, 2, WIN], f32))
        om = ctx.enter_context(nc.psum_tensor("om", [P, 2, WIN], f32))
        misc, opsum = om[:, 0, :], om[:, 1, :]

        Qd = nc.dram_tensor("q_parts", [3, P, T], bf16, kind="Internal").ap()
        Kd = nc.dram_tensor("k_parts", [3, P, NS], bf16, kind="Internal").ap()

        s_w, s_w2 = sem("first_weights_loaded"), sem("other_weights_loaded")
        s_stair = sem("staircase_rows_loaded")
        s_x = sem("x_loaded")
        s_out = sem("out_stored")
        s_init = sem("constants_set")
        s_qd = [sem(f"q_parts_stored_{w}") for w in range(NW)]
        s_kd = sem("k_parts_stored")
        s_qa = [sem(f"qa_loaded_{w}") for w in range(NW)]
        s_ka = sem("ka_loaded")
        s_mrow = sem("max_rows_loaded")
        s_wsplit, s_xh = sem("weights_split"), sem("xn2_high_ready")
        s_mfill, s_mfree = sem("misc_filled"), sem("misc_free")
        s_var1, s_rstd1, s_xn1 = sem("var1_ready"), sem("rstd1_ready"), sem("xn1_ready")
        s_pfill, s_pevac = sem("prep_bank_filled"), sem("prep_bank_evacuated")
        s_tails, s_sums, s_prod = sem("tails_v_ready"), sem("sums_v_ready"), sem("prod_ready")
        s_qsplit, s_ksplit = sem("q_split"), sem("k_split")
        s_maxin, s_maxed = sem("max_unit_filled"), sem("max_unit_reduced")
        s_mall, s_wrec = sem("group_maxima_ready"), sem("weight_factor_ready")
        s_msplit, s_mb = sem("max_split"), sem("max_rows_ready")
        s_expin, s_exped = sem("exp_unit_filled"), sem("exp_unit_done")
        s_pv, s_oevac = sem("pv_done"), sem("o_evacuated")
        s_td, s_et = sem("tail_diff_ready"), sem("tail_exp_ready")
        s_tv, s_den = sem("tail_v_weighted"), sem("denominators_ready")
        s_ao = sem("attn_out_ready")
        s_x1 = sem("x1_ready")
        s_var2, s_rstd2, s_xn2 = sem("var2_ready"), sem("rstd2_ready"), sem("xn2_ready")
        s_cp = sem("combine_ready")
        s_up, s_bc, s_dn = sem("up_done"), sem("weights_broadcast"), sem("down_done")
        s_relu, s_vw, s_h = sem("relu_done"), sem("weighted"), sem("hidden_ready")
        s_dev, s_y = sem("down_evacuated"), sem("y_ready")
        s_spare = sem("spare")
        s_cd1, s_cd2 = sem("dve_chain_prep"), sem("dve_chain_post")
        s_cd4, s_cd5 = sem("dve_chain_norm"), sem("dve_chain_parts")
        s_cp3, s_cp4 = sem("pool_chain_maxima"), sem("pool_chain_parts")
        s_cp1, s_cp2 = sem("pool_chain_prep"), sem("pool_chain_norm")

        N_FIRST, N_OTHER = 6, 6
        done_after = lambda st_: fill_no[st_] + 1
        parity = lambda n: mx[:, n % 2, :]

        block = ctx.enter_context(nc.Block())

        def batches(eng, body):
            with eng.Fori(0, B - 1) as b:
                body(b, False)
            body(B - 1, True)

        def tails(eng, chain, a):
            add = lambda dst, x, y: chain(eng.tensor_tensor(dst, x, y, ALU.add))
            for j in (1, 2):
                add(TAIL[:, a, :, j], TAIL[:, a, :, j], TAIL[:, a, :, j - 1])
            add(SUMS[:, a, :, 0:32], *(TAIL[:, a, :, j].rearrange("p (i s) -> p i s", i=NT) for j in (2, 3)))
            add(TAIL[:, a, :, 3], TAIL[:, a, :, 3], TAIL[:, a, :, 2])

        def sums(eng, chain, a):
            add = lambda dst, x, y: chain(eng.tensor_tensor(dst, x, y, ALU.add))
            at, n, L = 0, 32, BLK - 1
            while n > 1:
                pair = SUMS[:, a, :, at:at + n].rearrange("p i (s two) -> p i s two", two=2)
                add(SUMS[:, a, :, at + n:at + n + n // 2], pair[:, :, :, 0], pair[:, :, :, 1])
                at, n = at + n, n // 2
            half = SUMS[:, a, :, :].rearrange("p (i two) s -> p i two s", two=2)
            add(half[:, :, 1, L], half[:, :, 0, L - 1], half[:, :, 1, L - 1])
            for i in (0, 4):
                add(SUMS[:, a, i + 2, L:L + 1], SUMS[:, a, i + 1, L:L + 1], SUMS[:, a, i + 3, L:L + 1])
            add(SUMS[:, a, 4, L:L + 1], SUMS[:, a, 2, L:L + 1], SUMS[:, a, 6, L:L + 1])

        def by_head(w):
            t = slice(WT * w, WT * w + WT)
            return (lambda a: a[:, t, :].rearrange("p i (h d) -> p (i h) d", d=HS),
                    lambda a: a[:, t, :].rearrange("p i h -> p (i h)").unsqueeze(2).to_broadcast([P, WT * NH, HS]))

        def sets_out(w):
            return ATT[:, WT * w:WT * w + WT, :, 0:HS].rearrange("p i h d -> p (i h) d")

        def filled(eng, b, use):
            eng.wait_ge(s_mfill, b * MISCN + MISC[use] + 1)

        def freed(eng, b, use):
            eng.wait_ge(s_mfree, b * MISCN + MISC[use] + 2)

        @block.sync
        def _(sp):
            def load_x(p, first):
                if not first:
                    sp.wait_ge(s_x1, NW * p)
                src = x[bass.ds(p, 1)].rearrange("o (i p) c -> p (o i) c", p=P)
                sp.dma_start(X[:, :, :], src).then_inc(s_x, 16)

            def prep(p):
                sp.wait_ge(s_ksplit, p + 1)
                sp.dma_start(Kd.rearrange("a p s -> p a s"), Kparts[:, :, :]).then_inc(s_kd, 16)

                def store_q(w):
                    sp.wait_ge(s_qsplit, NW * p + w + 1)
                    win = slice(WIN * w, WIN * w + WIN)
                    sp.dma_start(Qd[:, :, win].rearrange("a p s -> p a s"), Qparts[:, :, win]).then_inc(s_qd[w], 16)

                def load_q(w):
                    sp.wait_ge(s_qd[w], 16 * p + 16)
                    for n, (part, _) in enumerate(PART_PAIRS):
                        r = ROW_PART + n * HS
                        src = Qd[part].rearrange("(h d) s -> d h s", d=HS)[:, :, WIN * w:WIN * w + WIN]
                        sp.dma_start(QA[r:r + HS, w, :, :], src).then_inc(s_qa[w], 16)

                store_q(0)
                sp.wait_ge(s_kd, 16 * p + 16)
                for n, (_, part) in enumerate(PART_PAIRS):
                    r = ROW_PART + n * HS
                    sp.dma_start(KA[r:r + HS, :, :], Kd[part].rearrange("(h d) s -> d h s", d=HS)).then_inc(s_ka, 16)
                load_q(0)
                store_q(1)
                load_q(1)

            def store_y(b, w):
                sp.wait_ge(s_y, NW * b + w + 1)
                dst = out[bass.ds(b, 1), WIN * w:WIN * w + WIN].rearrange("o (i p) c -> p (o i) c", p=P)
                sp.dma_start(dst, Y[:, w, :, :]).then_inc(s_out, 16)

            sp.sem_inc(s_out, 1)
            load_x(0, True)
            for dst, src in ((wqkv, w_qkv), (ident, ident_c), (head_sel, head_sel_c)):
                sp.dma_start(dst[:, :], src).then_inc(s_w, 16)
            for w in range(NW):
                sp.dma_start(QA[ROW_CONST:K_RAW, w, :, :], q_rows_c[:, WIN * w:WIN * w + WIN].unsqueeze(1)
                             .to_broadcast([N_CONST, NH, WIN])).then_inc(s_w, 16)
            sp.dma_start(KA[ROW_CONST:K_SUB, :, :], k_rows_c.unsqueeze(1).to_broadcast([K_SUB - ROW_CONST, NH, NS])).then_inc(s_w, 16)
            sp.dma_start(KA[0:N_STAIR, :, :], k_stair_c.unsqueeze(1).to_broadcast([N_STAIR, NH, NS])).then_inc(s_stair, 16)
            sp.dma_start(QA[0:N_STAIR, :, :, :].rearrange("k w h t -> k (w h) t"),
                         q_stair_c.unsqueeze(1).to_broadcast([N_STAIR, NW * NH, WIN])).then_inc(s_stair, 16)
            for dst, src in ((wproj[:, :], w_proj), (wgate[:, :], gate), (wup, up)):
                sp.dma_start(dst, src).then_inc(s_w2, 16)
            sp.dma_start(bias[:, :], e_bias.partition_broadcast(P)).then_inc(s_w2, 16)
            sp.dma_start(wdown[:, :, :], down.rearrange("(k p) c -> p k c", p=P)).then_inc(s_w2, 16)
            sp.dma_start(exp_sel[:, :, :], exp_sel_c).then_inc(s_w2, 16)
            prep(0)

            def maxima_rows(b, n):
                w, g = n // NG, n % NG
                sp.wait_ge(s_mb, b * NW * NG + n + 1)
                sp.dma_start(QA[K_RAW:K_SUB, w, G * g:G * g + G, :].rearrange("a h t -> a (h t)"), MB[:, :]).then_inc(s_mrow, 16)
            maxima_rows(0, 0)

            def body(b, last):
                for n in range(1, NW * NG):
                    maxima_rows(b, n)
                if not last:
                    load_x(b + 1, False)
                    prep(b + 1)
                store_y(b, 0)
                if not last:
                    maxima_rows(b + 1, 0)
                store_y(b, 1)
            batches(sp, body)
            sp.wait_ge(s_out, NW * 16 * B + 1)
            sp.wait_ge(s_kd, 16 * B)
            for w in range(NW):
                sp.wait_ge(s_qd[w], 16 * B)

        @block.gpsimd
        def _(pool):
            pool.memset(neg_half[:, :], -0.5).then_inc(s_init, 1)
            pool.memset(zeros[:, :], 0.0).then_inc(s_init, 1)
            pool.memset(VA[:, :, :, :], 0.0).then_inc(s_init, 1)
            pool.wait_ge(s_init, 3)
            pool.memset(VA[:, :, :, HS:HS + 1], 1.0).then_inc(s_init, 1)
            pool.memset(grp[:, :, 0:4], BIG).then_inc(s_init, 1)
            pool.memset(cand[:, :, 0:2], BIG).then_inc(s_init, 1)
            pool.memset(SUMS[:, :, 0, BLK - 1:BLK], 0.0).then_inc(s_init, 1)
            pool.wait_ge(s_w, 16 * N_FIRST)
            pool.tensor_copy(identb[:, :], ident[:, :]).then_inc(s_init, 1)

            chain1 = Chain(pool, s_cp1, 13, s_spare)
            chain2 = Chain(pool, s_cp2, 1, s_spare)
            chain3 = Chain(pool, s_cp3, 3, s_spare)
            chain4 = Chain(pool, s_cp4, 4, s_spare)

            def split(chain, parts, src, rem):
                none = zeros[:, 0:src.shape[-1]] if len(src.shape) == 2 else zeros[:, :].rearrange("p (i e) -> p i e", i=WT)
                chain(pool.tensor_tensor(parts[0], src, none, ALU.add))
                chain(pool.tensor_tensor(rem, src, parts[0], ALU.subtract))
                chain(pool.tensor_tensor(parts[1], rem, none, ALU.add))
                return pool.tensor_tensor(parts[2], rem, parts[1], ALU.subtract)

            def split_maxima(b, w, g):
                n = (b * NW + w) * NG + g
                chain3.begin(n)
                pool.wait_ge(s_mall, n + 1)
                if NG * w + g >= 2:
                    filled(pool, b, ("mT",) + divmod(NG * w + g - 2, NG))
                M = MALL[:, g, w, :, :].rearrange("p h i -> p (h i)")
                split(chain3, [MS[:, g % 2, a, :] for a in range(3)], M, mrem[:, :]).then_inc(s_msplit, 1)
                chain3.end()

            def prep_step(p, step):
                if step == "ln_stats":
                    pool.wait_ge(s_var1, p + 1)
                    pool.tensor_tensor(rstd[:, :], var[:, :], neg_half[:, :], ALU.pow).then_inc(s_rstd1, 1)
                elif step == "tails_v":
                    chain1.begin(p)
                    pool.wait_ge(s_pevac, p * FILLS + max(done_after("f6"), done_after("f7")))
                    tails(pool, chain1, 1)
                    pool.sem_inc(s_tails, 1)
                elif step == "sums_v":
                    sums(pool, chain1, 1)
                    pool.sem_inc(s_sums, 1)
                    chain1.end()

            def tail_weights(b, w):
                pool.wait_ge(s_et, NW * b + w + 1)
                heads, flat = by_head(w)
                pool.tensor_tensor(heads(VW), heads(VTL), flat(ET), ALU.mult).then_inc(s_tv, 1)

            def post_step(b, w, step):
                if step == "norm" and w == 0:
                    heads, flat = by_head(w)
                    chain2.begin(b)
                    freed(pool, b, ("oT", w, NG - 1))
                    pool.wait_ge(s_tv, NW * b + w + 1)
                    chain2(pool.tensor_tensor(heads(VW), heads(VW), sets_out(w), ALU.add))
                    pool.wait_ge(s_den, b + 1)
                    pool.tensor_tensor(heads(AO), heads(VW), flat(DEN), ALU.mult).then_inc(s_ao, 1)
                elif step == "parts" and w == 0:
                    chain4.begin(b)
                    t = slice(0, WT)
                    pool.wait_ge(s_wrec, NW * b + 1)
                    chain4(pool.tensor_tensor(WSEL[:, t, :], WSEL[:, t, :], wsum[:, t].unsqueeze(2).to_broadcast([P, WT, NE]), ALU.mult))
                    split(chain4, [CP[:, t, a, :] for a in range(3)], WSEL[:, t, :], wrem[:, t, :]).then_inc(s_cp, 1)
                    chain4.end()
                elif step == "stats":
                    pool.wait_ge(s_var2, NW * b + w + 1)
                    pool.tensor_tensor(rstd[:, WT * w:WT * w + WT], var[:, WT * w:WT * w + WT], neg_half[:, 0:WT],
                                       ALU.pow).then_inc(s_rstd2, 1)

            def body(b, last):
                for kind, w, g, n in ORDER:
                    if kind == "mfin":
                        split_maxima(b, w, g)
                    elif kind == "tail":
                        tail_weights(b, w)
                    elif kind == "post":
                        post_step(b, w, n)
                for u in range(UNITS):
                    for step in POST_AT.get(u, []):
                        post_step(b, 1, step)
                    if not last:
                        for step in PREP_AT.get(u, []):
                            prep_step(b + 1, step)
                    routed = (u // NCH) * 16 + u % NCH - 2
                    if u >= 4:
                        pool.wait_ge(s_dn, b * UNITS + u - 3)
                    if CHUNKS[u % NCH] < 16:
                        pool.wait_ge(s_vw, b * 32 + routed + 1)
                        src = V
                    else:
                        pool.wait_ge(s_relu, b * UNITS + u + 1)
                        src = R
                    pool.tensor_tensor(H[:, u % 4, :], src[:, u % 4, :], R[:, u % 4, :], ALU.mult).then_inc(s_h, 1)
                    if not last:
                        lead_maxima(b + 1, LEAD_AT.get(u, []))
                if not last:
                    for u in range(UNITS, FFN_SLOTS):
                        lead_maxima(b + 1, LEAD_AT.get(u, []))

            def lead_maxima(b, events):
                for kind, w, g, n in events:
                    if kind == "mfin":
                        split_maxima(b, w, g)

            for step in PREP_ALL:
                prep_step(0, step)
            lead_maxima(0, LEAD)
            batches(pool, body)

        @block.scalar
        def _(act):
            def prep_step(p, step):
                if step[0] != "f":
                    return
                n = fill_no[step]
                bank = parity(n)
                act.wait_ge(s_pfill, p * FILLS + n + 1)
                if step in ("f0", "f1"):
                    k = int(step[1])
                    ins = act.activation(XNT[:, WIN * k:WIN * k + WIN], bank, ACT.Copy)
                elif step in ("f2", "f3"):
                    k = int(step[1]) - 2
                    ins = act.activation(QT[:, WIN * k:WIN * k + WIN], bank, ACT.Copy)
                elif step in ("f4", "f5", "f6", "f7"):
                    k = int(step[1]) - 4
                    ins = act.activation(TAIL[:, k // 2, P * (k % 2):P * (k % 2) + P, :],
                                         bank.rearrange("p (n j) -> p n j", j=4), ACT.Copy)
                elif step == "f8":
                    ins = act.activation(VA[:, :, :, 0:HS], bank.rearrange("p (c h d) -> p c h d", c=4, d=HS), ACT.Copy)
                elif step in ("f9", "f10"):
                    k = int(step[1:]) - 9
                    ins = act.activation(VTL[:, 4 * k:4 * k + 4, :], bank.rearrange("p (i c) -> p i c", i=4), ACT.Copy)
                else:
                    ins = act.activation(TLG[:, :, :], bank[:, 0:P].rearrange("p (i h) -> p i h", i=NT), ACT.Copy)
                ins.then_inc(s_pevac, 1)

            def post_step(b, w, step):
                t0 = WIN * w
                if step not in ("aT", "xT", "logits", "cT"):
                    return
                filled(act, b, (step, w, 0))
                if step == "aT":
                    ins = act.activation(ATTT[:, t0:t0 + WIN], misc, ACT.Copy)
                elif step == "xT":
                    act.activation(XH[:, t0:t0 + WIN], misc, ACT.Copy).then_inc(s_xh, 1)
                    return
                elif step == "logits":
                    ins = act.activation(SCO[:, WT * w:WT * w + WT, :], misc[:, 0:WT * NE].rearrange("p (i e) -> p i e", i=WT),
                                         ACT.Exp, scale=-1.0)
                else:
                    ins = act.activation(CT[:, t0:t0 + WIN], misc.bitcast(bf16)[0:3 * NE, 0:WIN], ACT.Copy)
                ins.then_inc(s_mfree, 1)

            def attend(b):
                for kind, w, g, n in ORDER:
                    if kind == "exp":
                        c, h0, nh, t0, nt = EXP_UNITS[w][n]
                        u = pos_exp(w, g, n)
                        k = pos_pv(w, g, [x[0] for x in PV_STEPS[w]].index(c))
                        act.wait_ge(s_expin, b * EXPN + u + 1)
                        if k >= NPT:
                            act.wait_ge(s_pv, b * PVN + k - NPT + 1)
                        src = st[:, 2 * (u % 2):2 * (u % 2) + 2, :].rearrange("p k (h t) -> p (k h) t", t=nt)
                        act.activation(PT[:, k % NPT, h0:h0 + nh, 0:nt], src, ACT.Exp, scale=SCALE).then_inc(s_exped, 1)
                    elif kind == "oevac":
                        act.wait_ge(s_pv, b * PVN + pos_pv(w, g, len(PV_STEPS[w]) - 1) + 1)
                        if (w, g) != (0, 0):
                            filled(act, b, ("oT", w, g - 1) if g else ("oT", w - 1, NG - 1))
                        act.activation(OS[:, :], opsum, ACT.Copy).then_inc(s_oevac, 1)
                    elif kind == "tail":
                        act.wait_ge(s_td, NW * b + w + 1)
                        act.activation(ET[:, WT * w:WT * w + WT, :], TD[:, WT * w:WT * w + WT, :], ACT.Exp,
                                       scale=SCALE).then_inc(s_et, 1)
                    elif kind == "post":
                        post_step(b, w, n)

            def down_evac(b, w):
                act.wait_ge(s_dn, b * UNITS + NCH * (w + 1))
                act.activation(OT[:, w, :], opsum, ACT.Copy).then_inc(s_dev, 1)

            def ffn(b, last):
                for u in range(UNITS):
                    for step in POST_AT.get(u, []):
                        post_step(b, 1, step)
                    if not last:
                        for step in PREP_AT.get(u, []):
                            prep_step(b + 1, step)
                    act.wait_ge(s_up, b * UNITS + u + 1)
                    if u >= 4:
                        act.wait_ge(s_h, b * UNITS + u - 3)
                    act.activation(R[:, u % 4, :], st[:, u % 2, :], ACT.Relu).then_inc(s_relu, 1)
                    if u == NCH + LAG - 1:
                        down_evac(b, 0)
                down_evac(b, 1)

            act.wait_ge(s_init, 7)
            for step in PREP_ALL:
                if step == "f11":
                    act.wait_ge(s_w2, 16 * N_OTHER)
                    act.activation(WUH[:, :], wup, ACT.Copy).then_inc(s_wsplit, 1)
                    act.activation(WGH[:, :], wgate[:, :], ACT.Copy).then_inc(s_wsplit, 1)
                prep_step(0, step)
            act.wait_ge(s_wsplit, 4)

            def body(b, last):
                attend(b)
                ffn(b, last)
            batches(act, body)

        @block.tensor
        def _(pe):
            def use_misc(b, use):
                pe.wait_ge(s_mfree, b * MISCN + MISC[use] + 1)

            def prep_step(p, step, first):
                if step[0] != "f":
                    return
                n = fill_no[step]
                bank = parity(n)
                if n >= 2:
                    pe.wait_ge(s_pevac, p * FILLS + n - 1)
                elif not first:
                    pe.wait_ge(s_maxed, p * MAXN)
                if step in ("f0", "f1"):
                    k = int(step[1])
                    pe.wait_ge(s_xn1, p * NT + WT * k + WT)
                    for i in range(WT):
                        ins = pe.transpose(bank[:, P * i:P * i + P], XN[:, WT * k + i, :], ident[:, :])
                elif step in ("f2", "f3", "f4", "f5", "f6", "f7"):
                    k = int(step[1]) - 2
                    pe.wait_ge(s_pevac, p * FILLS + done_after("f1"))
                    ins = pe.matmul(bank, wqkv[:, C * (k // 2):C * (k // 2) + C],
                                    XNT[:, WIN * (k % 2):WIN * (k % 2) + WIN], start=True, stop=True)
                elif step == "f8":
                    pe.wait_ge(s_sums, p + 1)
                    for c in range(4):
                        ins = pe.transpose(bank[:, P * c:P * c + P],
                                           SUMS[:, 1, 2 * c:2 * c + 2, :].rearrange("p a s -> p (a s)"), ident[:, :])
                elif step in ("f9", "f10"):
                    k = int(step[1:]) - 9
                    pe.wait_ge(s_tails, p + 1)
                    for i in range(4):
                        v = TAIL[:, 1, 32 * (4 * k + i):32 * (4 * k + i) + 32, :].rearrange("p n j -> p (n j)")
                        ins = pe.transpose(bank[:, P * i:P * i + P], v, ident[:, :])
                else:
                    pe.wait_ge(s_prod, p + 1)
                    for i in range(NT):
                        ins = pe.matmul(bank[:, NH * i:NH * i + NH], PROD[:, P * i:P * i + P], head_sel[:, :],
                                        start=True, stop=True)
                ins.then_inc(s_pfill, 1)

            def post_step(b, w, step):
                if step not in ("aT", "proj", "xT", "logits", "cT"):
                    return
                use_misc(b, (step, w, 0))
                if step == "aT":
                    pe.wait_ge(s_ao, NW * b + w + 1)
                    for i in range(WT):
                        ins = pe.transpose(misc[:, P * i:P * i + P], AO[:, WT * w + i, :], ident[:, :])
                elif step == "proj":
                    freed(pe, b, ("aT", w, 0))
                    for i in range(WT):
                        t0 = P * (WT * w + i)
                        ins = pe.matmul(misc[:, P * i:P * i + P], ATTT[:, t0:t0 + P], wproj[:, :], start=True, stop=True)
                elif step == "xT":
                    pe.wait_ge(s_xn2, b * NT + WT * w + WT)
                    for i in range(WT):
                        ins = pe.transpose(misc[:, P * i:P * i + P], XN[:, WT * w + i, :], ident[:, :])
                elif step == "logits":
                    freed(pe, b, ("xT", w, 0))
                    for i in range(WT):
                        t0 = P * (WT * w + i)
                        pairs = [(xa, wa) for xa in (XH, XL) for wa in (WGH, WGL)]
                        for n, (xa, wa) in enumerate(pairs):
                            ins = pe.matmul(misc[:, NE * i:NE * i + NE], xa[:, t0:t0 + P], wa[:, :],
                                            start=(n == 0), stop=(n == 3), skip_group_check=True)
                else:
                    pe.wait_ge(s_cp, NW * b + w + 1)
                    for i in range(WT):
                        ins = pe.transpose(misc.bitcast(bf16)[0:3 * NE, P * i:P * i + P],
                                           CP[:, WT * w + i, :, :].rearrange("p a e -> p (a e)"), identb[:, :])
                ins.then_inc(s_mfill, 1)

            def max_unit(b, w, g, n):
                i, h0, nh = MAX_UNITS[w][n]
                u = pos_max(w, g, n)
                if u >= 2:
                    pe.wait_ge(s_maxed, b * MAXN + u - 1)
                else:
                    pe.wait_ge(s_pevac, (b + 1) * FILLS)
                    pe.wait_ge(s_ka, (b + 1) * len(PART_PAIRS) * 16)
                    pe.wait_ge(s_qa[0], (b + 1) * len(PART_PAIRS) * 16)
                if u == pos_max(1, 0, 0):
                    pe.wait_ge(s_qa[1], (b + 1) * len(PART_PAIRS) * 16)
                ns = BLK * (i + 1)
                for k in range(nh):
                    h = G * g + h0 + k
                    for r0, s0, s1 in ((ROW_PART, 0, ns - BLK), (0, ns - BLK, ns))[i == 0:]:
                        ins = pe.matmul(mx[:, u % 2, ns * k + s0:ns * k + s1],
                                        QA[r0:K_RAW, w, h, P * (i % WT):P * (i % WT) + P], KA[r0:K_RAW, h, s0:s1],
                                        start=True, stop=True)
                ins.then_inc(s_maxin, 1)

            def maxima_transpose(b, w, g):
                use_misc(b, ("mT", w, g))
                pe.wait_ge(s_msplit, (b * NW + w) * NG + g + 1)
                pe.sem_inc(s_spare, 1)
                pe.transpose(misc.bitcast(bf16)[0:3 * G * WT, 0:P], MS[:, g % 2, :, :].rearrange("p a m -> p (a m)"),
                             identb[:, :]).then_inc(s_mfill, 1)

            def half(kind, n):
                return range(n // 2) if kind[-1] == "1" else range(n // 2, n)

            def attend(b):
                for kind, w, g, n in ORDER:
                    if kind == "max":
                        max_unit(b, w, g, n)
                    elif kind == "mT":
                        maxima_transpose(b, w, g)
                    elif kind in ("exp1", "exp"):
                        c, h0, nh, t0, nt = EXP_UNITS[w][n]
                        u = pos_exp(w, g, n)
                        if kind == "exp1":
                            if n == 0:
                                pe.wait_ge(s_mrow, ((b * NW + w) * NG + g + 1) * 16)
                            if u >= 2:
                                pe.wait_ge(s_exped, b * EXPN + u - 1)
                        own = c // 2 == w
                        if own:
                            parts = [(0, t0, t0 + 2 * P)]
                            if nt > 2 * P:
                                parts.append((ROW_PART, t0 + 2 * P, t0 + nt))
                        else:
                            parts = [(ROW_PART, t0, t0 + nt)]
                        for k in half(kind, nh):
                            h = G * g + h0 + k
                            for r0, a0, a1 in parts:
                                at = k * nt + a0 - t0
                                ins = pe.matmul(st[:, 2 * (u % 2) + at // WIN, at % WIN:at % WIN + a1 - a0],
                                                KA[r0:K_SUB, h, P * c:P * c + P], QA[r0:K_SUB, w, h, a0 - WIN * w:a1 - WIN * w],
                                                start=True, stop=True)
                        if kind == "exp":
                            ins.then_inc(s_expin, 1)
                    elif kind in ("pv1", "pv"):
                        c, t0, nt, need = PV_STEPS[w][n]
                        k = pos_pv(w, g, n)
                        if kind == "pv1":
                            pe.wait_ge(s_exped, b * EXPN + pos_exp(w, g, need))
                            o = NG * w + g
                            if c == 0 and o:
                                pe.wait_ge(s_oevac, b * NW * NG + o)
                            elif c == 0:
                                pe.wait_ge(s_dev, NW * b + 1)
                        for h in half(kind, G):
                            ins = pe.matmul(opsum[32 * h:32 * h + 32, t0 - WIN * w:t0 - WIN * w + nt],
                                            VA[:, c, G * g + h, :], PT[:, k % NPT, h, 0:nt],
                                            start=(c == 0), stop=(c == 2 * w + 1), skip_group_check=True)
                        if kind == "pv":
                            ins.then_inc(s_pv, 1)
                    elif kind == "oT":
                        use_misc(b, ("oT", w, g))
                        pe.wait_ge(s_oevac, (b * NW + w) * NG + g + 1)
                        for i in range(WT):
                            ins = pe.transpose(misc[:, P * i:P * i + P], OS[:, P * i:P * i + P], ident[:, :])
                        ins.then_inc(s_mfill, 1)
                    elif kind == "post":
                        post_step(b, w, n)

            def y_transpose(b, w, last):
                if w and last:
                    pe.wait_ge(s_mfree, (b + 1) * MISCN + 1)
                else:
                    use_misc(b + w, ("yT", w, 0))
                pe.wait_ge(s_dev, NW * b + w + 2)
                for i in range(WT):
                    ins = pe.transpose(misc[:, P * i:P * i + P], OT[:, w, P * i:P * i + P], ident[:, :])
                ins.then_inc(s_mfill, 1)

            def ffn(b, last):
                routed = 0
                for v in range(FFN_SLOTS):
                    if v < UNITS:
                        for step in POST_AT.get(v, []):
                            post_step(b, 1, step)
                        if not last:
                            for step in PREP_AT.get(v, []):
                                prep_step(b + 1, step, False)
                        w, k = v // NCH, CHUNKS[v % NCH]
                        if v == 0:
                            pe.wait_ge(s_wsplit, 4)
                            freed(pe, b, ("xT", 0, 0))
                            pe.wait_ge(s_exped, (b + 1) * EXPN)
                        if v == NCH:
                            freed(pe, b, ("xT", 1, 0))
                        if v >= 2:
                            pe.wait_ge(s_relu, b * UNITS + v - 1)
                        for n, (wa, xa) in enumerate(((WUH, XH), (WUH, XL), (WUL, XH))):
                            ins = pe.matmul(st[:, v % 2, :], wa[:, P * k:P * k + P], xa[:, WIN * w:WIN * w + WIN],
                                            start=(n == 0), stop=(n == 2))
                        ins.then_inc(s_up, 1)
                        if k < 16:
                            if routed % 16 == 0:
                                freed(pe, b, ("cT", w, 0))
                            if routed >= 2:
                                pe.wait_ge(s_vw, b * 32 + routed - 1)
                            pe.matmul(st[:, 2 + routed % 2, :], exp_sel[:, k, :], CT[:, WIN * w:WIN * w + WIN],
                                      start=True, stop=True).then_inc(s_bc, 1)
                            routed += 1
                    if LAG <= v < UNITS + LAG:
                        d = v - LAG
                        w, n = d // NCH, d % NCH
                        if d == 0:
                            pe.wait_ge(s_oevac, (b + 1) * NW * NG)
                        if d == NCH:
                            pe.wait_ge(s_dev, NW * b + 2)
                        pe.wait_ge(s_h, b * UNITS + d + 1)
                        pe.matmul(opsum, wdown[:, CHUNKS[n], :], H[:, d % 4, :],
                                  start=(n == 0), stop=(n == NCH - 1)).then_inc(s_dn, 1)
                    if v == Y0_AT:
                        y_transpose(b, 0, last)
                    if not last:
                        for kind, w, g, n in LEAD_AT.get(v, []):
                            if kind == "max":
                                max_unit(b + 1, w, g, n)
                            elif kind == "mT":
                                maxima_transpose(b + 1, w, g)
                y_transpose(b, 1, last)

            pe.wait_ge(s_w, 16 * N_FIRST)
            pe.wait_ge(s_init, 8)
            for step in PREP_ALL:
                prep_step(0, step, True)
            pe.wait_ge(s_stair, 32)
            for kind, w, g, n in LEAD:
                if kind == "max":
                    max_unit(0, w, g, n)
                elif kind == "mT":
                    maxima_transpose(0, w, g)
            pe.sem_inc(s_mfill, 1)

            def body(b, last):
                attend(b)
                ffn(b, last)
            batches(pe, body)

        @block.vector
        def _(dve):
            chain1 = Chain(dve, s_cd1, 24, s_spare)
            chain2 = Chain(dve, s_cd2, 26, s_spare)
            chain4 = Chain(dve, s_cd4, 4, s_spare)
            chain5 = Chain(dve, s_cd5, 4, s_spare)

            def ln_stats(src, chain, tiles, s_var):
                for i in tiles:
                    ins = dve.bn_stats(stats[:, i, :], src[:, i, :])
                chain.alone(ins)
                for i in tiles:
                    ins = dve.bn_aggr(mv[:, i, :], stats[:, i, :])
                chain(ins)
                t = slice(tiles[0], tiles[-1] + 1)
                dve.tensor_scalar(var[:, t], mv[:, t, 1], 1e-5, None, ALU.add).then_inc(s_var, 1)

            def ln_apply(src, tiles, s_rstd, v, s_xn):
                dve.wait_ge(s_rstd, v)
                for i in tiles:
                    dve.tensor_scalar(XN[:, i, :], src[:, i, :], mv[:, i, 0:1], rstd[:, i:i + 1],
                                      ALU.subtract, ALU.mult).then_inc(s_xn, 1)

            def prep_step(p, step, first):
                if step == "ln_stats":
                    chain1.begin(p)
                    dve.wait_ge(s_x, 16 * p + 16)
                    ln_stats(X, chain1, range(NT), s_var1)
                elif step in ("ln_apply0", "ln_apply1"):
                    t0 = WT * int(step[-1])
                    ln_apply(X, range(t0, t0 + WT), s_rstd1, p + 1, s_xn1)
                elif step == "tails_k":
                    dve.wait_ge(s_pevac, p * FILLS + max(done_after("f4"), done_after("f5")))
                    tails(dve, chain1, 0)
                elif step == "sums_k":
                    sums(dve, chain1, 0)
                elif step == "ksplit":
                    if not first:
                        dve.wait_ge(s_kd, 16 * p)
                    K = SUMS[:, 0, :, :].rearrange("p i s -> p (i s)")
                    chain1(dve.tensor_copy(Kparts[:, 0, :], K))
                    chain1(dve.tensor_tensor(krem, K, Kparts[:, 0, :], ALU.subtract))
                    chain1(dve.tensor_copy(Kparts[:, 1, :], krem))
                    dve.tensor_tensor(Kparts[:, 2, :], krem, Kparts[:, 1, :], ALU.subtract).then_inc(s_ksplit, 1)
                elif step in ("qsplit0", "qsplit1"):
                    w = int(step[-1])
                    win = slice(WIN * w, WIN * w + WIN)
                    dve.wait_ge(s_pevac, p * FILLS + done_after(f"f{2 + w}"))
                    if not first:
                        dve.wait_ge(s_qd[w], 16 * p)
                    chain1(dve.tensor_copy(Qparts[:, 0, win], QT[:, win]))
                    chain1(dve.tensor_tensor(qrem[:, win], QT[:, win], Qparts[:, 0, win], ALU.subtract))
                    chain1(dve.tensor_copy(Qparts[:, 1, win], qrem[:, win]))
                    dve.tensor_tensor(Qparts[:, 2, win], qrem[:, win], Qparts[:, 1, win], ALU.subtract).then_inc(s_qsplit, 1)
                elif step == "prod":
                    dve.wait_ge(s_pevac, p * FILLS + max(done_after("f6"), done_after("f7")))
                    dve.tensor_tensor(PROD[:, :], QT[:, :], TAIL[:, 0, :, :].rearrange("p n j -> p (n j)"),
                                      ALU.mult).then_inc(s_prod, 1)
                    chain1.end()

            def max_event(b, kind, w, g, n):
                if kind == "max":
                    i, h0, nh = MAX_UNITS[w][n]
                    u = pos_max(w, g, n)
                    ns = BLK * (i + 1)
                    dve.wait_ge(s_maxin, b * MAXN + u + 1)
                    dve.reduce_max(MXR[:, g, i, h0:h0 + nh], mx[:, u % 2, 0:ns * nh].rearrange("p (h s) -> p h s", s=ns),
                                   AX.X).then_inc(s_maxed, 1)
                elif kind == "mT":
                    filled(dve, b, ("mT", w, g))
                    if (w, g) != (0, 0):
                        dve.wait_ge(s_mrow, ((b * NW + w) * NG + g) * 16)
                    dve.tensor_copy(MB[:, :], misc.bitcast(bf16)[0:3 * G * WT, 0:P]).then_inc(s_mb, 1)
                    dve.wait_ge(s_mb, (b * NW + w) * NG + g + 1)
                    dve.sem_inc(s_mfree, 1)
                elif kind == "mfin":
                    t = slice(WT * w, WT * w + WT)
                    dve.wait_ge(s_maxed, b * MAXN + pos_max(w, g, len(MAX_UNITS[w]) - 1) + 1)
                    dve.tensor_tensor(MALL[:, g, w, :, :], MXR[:, g, t, :].rearrange("p i h -> p h i"),
                                      TLG[:, t, G * g:G * g + G].rearrange("p i h -> p h i"), ALU.max).then_inc(s_mall, 1)

            def attend(b):
                for kind, w, g, n in ORDER:
                    if kind in ("max", "mfin", "mT"):
                        max_event(b, kind, w, g, n)
                    elif kind == "tail":
                        t = slice(WT * w, WT * w + WT)
                        dve.wait_ge(s_mall, (b * NW + w) * NG + NG)
                        dve.tensor_tensor(TD[:, t, :].rearrange("p i (g h) -> p i g h", g=NG),
                                          TLG[:, t, :].rearrange("p i (g h) -> p i g h", g=NG),
                                          MALL[:, :, w, :, :].rearrange("p g h i -> p i g h"), ALU.subtract).then_inc(s_td, 1)
                    elif kind == "oT":
                        filled(dve, b, ("oT", w, g))
                        dve.tensor_copy(ATT[:, WT * w:WT * w + WT, G * g:G * g + G, :],
                                        misc.rearrange("p (i h d) -> p i h d", i=WT, h=G)[:, :, :, 0:HS + 1]).then_inc(s_mfree, 1)
                    elif kind == "post":
                        post_step(b, w, n)

            def post_step(b, w, step):
                t = slice(WT * w, WT * w + WT)
                if step == "norm":
                    chain2.begin(NW * b + w)
                    if w == 0:
                        chain4.begin(b)
                    heads, flat = by_head(w)
                    dve.wait_ge(s_et, NW * b + w + 1)
                    freed(dve, b, ("oT", w, NG - 1))
                    chain4(dve.tensor_tensor(DEN[:, t, :], ATT[:, t, :, HS], ET[:, t, :], ALU.add))
                    ins = dve.reciprocal(DEN[:, t, :], DEN[:, t, :])
                    if w == 0:
                        ins.then_inc(s_den, 1)
                        return
                    chain4(ins)
                    dve.wait_ge(s_tv, NW * b + w + 1)
                    chain4(dve.tensor_tensor(heads(VW), heads(VW), sets_out(w), ALU.add))
                    dve.tensor_tensor(heads(AO), heads(VW), flat(DEN), ALU.mult).then_inc(s_ao, 1)
                elif step == "proj":
                    filled(dve, b, ("proj", w, 0))
                    chain2(dve.tensor_tensor(X1[:, t, :], misc.rearrange("p (i c) -> p i c", i=WT), X[:, t, :], ALU.add))
                    dve.sem_inc(s_mfree, 1)
                    dve.sem_inc(s_x1, 1)
                elif step == "stats":
                    ln_stats(X1, chain2, range(WT * w, WT * w + WT), s_var2)
                elif step == "xT":
                    dve.wait_ge(s_xh, NW * b + w + 1)
                    win = slice(WIN * w, WIN * w + WIN)
                    dve.tensor_tensor(XL[:, win], misc, XH[:, win].bitcast(f32), ALU.subtract).then_inc(s_mfree, 1)
                elif step == "apply":
                    ln_apply(X1, range(WT * w, WT * w + WT), s_rstd2, NW * b + w + 1, s_xn2)
                elif step == "score":
                    freed(dve, b, ("logits", w, 0))
                    chain2(dve.tensor_scalar(SCO[:, t, :], SCO[:, t, :], 1.0, None, ALU.add))
                    chain2(dve.reciprocal(SCO[:, t, :], SCO[:, t, :]))
                    chain2(dve.tensor_tensor(SCB[:, t, :], SCO[:, t, :], bias[:, :].unsqueeze(1).to_broadcast([P, WT, NE]), ALU.add))
                elif step == "pairs":
                    four = SCB[:, t, :].rearrange("p i (g two k) -> p (i g) two k", g=NGRP, two=2)
                    hv, lv = hi2[:, 0, t, :, :], hi2[:, 1, t, :, :]
                    for v, op in ((hv, ALU.max), (lv, ALU.min)):
                        chain2(dve.tensor_tensor(v.rearrange("p i g k -> p (i g) k"), four[:, :, 0, :], four[:, :, 1, :], op))
                    first, second, third = (wrem[:, t, NGRP * k:NGRP * k + NGRP] for k in range(3))
                    chain2(dve.tensor_tensor(first, hv[:, :, :, 0], hv[:, :, :, 1], ALU.max))
                    chain2(dve.tensor_tensor(second, hv[:, :, :, 0], hv[:, :, :, 1], ALU.min))
                    chain2(dve.tensor_tensor(third, lv[:, :, :, 0], lv[:, :, :, 1], ALU.max))
                    chain2(dve.tensor_tensor(second, second, third, ALU.max))
                    chain2.alone(dve.tensor_tensor(grp[:, t, 4:], first, second, ALU.add))
                elif step == "groups":
                    choose(w, grp, grpo)
                    chain2(dve.tensor_tensor(gmask[:, t, :], grpo[:, t, 4:], grp[:, t, 4:], ALU.not_equal))
                    chain2(dve.tensor_tensor(WSEL[:, t, :].rearrange("p i (g k) -> p (i g) k", k=GE),
                                             SCB[:, t, :].rearrange("p i (g k) -> p (i g) k", k=GE),
                                             gmask[:, t, :].rearrange("p i g -> p (i g)").unsqueeze(2).to_broadcast([P, WT * NGRP, GE]), ALU.mult))
                    chain2.alone(dve.tensor_scalar(cand[:, t, 2:], WSEL[:, t, :], 0.0, None, ALU.add))
                elif step == "experts":
                    choose(w, cand, cando)
                    chain2(dve.tensor_tensor(WSEL[:, t, :], cando[:, t, 2:], cand[:, t, 2:], ALU.not_equal))
                    chain2(dve.tensor_tensor(WSEL[:, t, :], WSEL[:, t, :], SCO[:, t, :], ALU.mult))
                    chain2(dve.reduce_sum(wsum[:, t], WSEL[:, t, :], AX.X))
                elif step == "weights":
                    chain2(dve.tensor_scalar(wsum[:, t], wsum[:, t], 1e-20, None, ALU.add))
                    chain2(dve.reciprocal(wsum[:, t], wsum[:, t]))
                    chain2(dve.tensor_scalar(wsum[:, t], wsum[:, t], ROUTED_SCALE, None, ALU.mult))
                    chain2.end()
                    dve.sem_inc(s_wrec, 1)
                elif step == "parts" and w == 1:
                    chain5.begin(b)
                    chain5(dve.tensor_tensor(WSEL[:, t, :], WSEL[:, t, :], wsum[:, t].unsqueeze(2).to_broadcast([P, WT, NE]), ALU.mult))
                    chain5(dve.tensor_copy(CP[:, t, 0, :], WSEL[:, t, :]))
                    chain5(dve.tensor_tensor(wrem[:, t, :], WSEL[:, t, :], CP[:, t, 0, :], ALU.subtract))
                    chain5(dve.tensor_copy(CP[:, t, 1, :], wrem[:, t, :]))
                    chain5.end()
                    dve.tensor_tensor(CP[:, t, 2, :], wrem[:, t, :], CP[:, t, 1, :], ALU.subtract).then_inc(s_cp, 1)

            def choose(w, values, replaced):
                for i in range(WT * w, WT * w + WT):
                    ins = dve.max(top8[:, i, :], values[:, i, :])
                chain2.alone(ins)
                for i in range(WT * w, WT * w + WT):
                    ins = dve.match_replace(replaced[:, i, :], top8[:, i, :], values[:, i, :], -3.0 * BIG)
                chain2(ins)

            def finish(b, w, last):
                if w and last:
                    dve.wait_ge(s_mfill, (b + 1) * MISCN + 1)
                else:
                    filled(dve, b + w, ("yT", w, 0))
                dve.wait_ge(s_out, NW * 16 * b + 1)
                dve.tensor_tensor(Y[:, w, :, :], misc.rearrange("p (i c) -> p i c", i=WT),
                                  X1[:, WT * w:WT * w + WT, :], ALU.add).then_inc(s_y, 1)
                dve.wait_ge(s_y, NW * b + w + 1)
                dve.sem_inc(s_mfree, 1)

            def ffn(b, last):
                routed = 0
                for v in range(FFN_SLOTS):
                    if v < UNITS:
                        for step in POST_AT.get(v, []):
                            post_step(b, 1, step)
                        if not last:
                            for step in PREP_AT.get(v, []):
                                prep_step(b + 1, step, False)
                    u = v - 1
                    if 0 <= u < UNITS and CHUNKS[u % NCH] < 16:
                        dve.wait_ge(s_relu, b * UNITS + u + 1)
                        dve.wait_ge(s_bc, b * 32 + routed + 1)
                        if u >= 4:
                            dve.wait_ge(s_h, b * UNITS + u - 3)
                        dve.tensor_tensor(V[:, u % 4, :], R[:, u % 4, :], st[:, 2 + routed % 2, :], ALU.mult).then_inc(s_vw, 1)
                        routed += 1
                    if v == Y0_AT + 1:
                        finish(b, 0, last)
                    if not last:
                        for ev in LEAD_AT.get(v, []):
                            max_event(b + 1, *ev)
                finish(b, 1, last)

            dve.sem_inc(s_mfree, 1)
            dve.sem_inc(s_dev, 1)
            dve.wait_ge(s_init, 7)
            for step in PREP_ALL:
                prep_step(0, step, True)
            dve.wait_ge(s_wsplit, 2)
            for hi, lo, full in ((WUH, WUL, wup), (WGH, WGL, wgate[:, :])):
                dve.tensor_tensor(lo[:, :], full, hi[:, :].bitcast(f32), ALU.subtract).then_inc(s_wsplit, 1)
            for ev in LEAD:
                max_event(0, *ev)
            dve.sem_inc(s_mfree, 1)
            dve.wait_ge(s_w2, 16 * N_OTHER)

            def body(b, last):
                attend(b)
                ffn(b, last)
            batches(dve, body)


_INS = ["x", "w_qkv", "w_proj", "gate", "e_bias", "up", "down", "ident", "head_sel", "q_stair", "k_stair",
        "q_rows", "k_rows", "exp_sel"]


def layout(i):
    import numpy as np
    from concourse import mybir
    b16 = mybir.dt.np(mybir.dt.bfloat16)
    d = {k: np.asarray(v) for k, v in i.items()}
    up = np.concatenate([d["L0_ffn_up_w"].reshape(NE * 64, C), d["L0_ffn_shared_up_w"]], 0)
    down = np.concatenate([d["L0_ffn_down_w"].transpose(0, 2, 1).reshape(NE * 64, C), d["L0_ffn_shared_down_w"].T], 0)
    last = []
    n, size = 32, 4
    while n >= 1:
        last += [size * (k + 1) - 1 for k in range(n)]
        n, size = n // 2, size * 2
    last = np.array(last + [P - 1])
    t = np.arange(WIN) % (2 * P)
    q_stair = np.where(t[None, :] < 4 * np.arange(N_STAIR)[:, None] + 3, -BIG, 0.0)
    k_stair = np.zeros((N_STAIR, NT // 2, 2, BLK), np.float32)
    for odd in range(2):
        for slot in range(BLK - 1 + odd):
            k_stair[(last[slot] + P * odd) // 4, :, odd, slot] = 1.0
    k_stair = k_stair.reshape(N_STAIR, NS)
    tt = np.arange(T)
    q_rows = np.stack([tt >= 0, tt < 511, tt < 1023]).astype(np.float32)
    k_rows = np.zeros((K_SUB - ROW_CONST, NS), np.float32)
    k_rows[0, BLK - 1] = -BIG
    k_rows[1, 2 * BLK + BLK - 1] = -BIG
    k_rows[2, [4 * BLK + BLK - 1, 6 * BLK + BLK - 1]] = -BIG
    k_rows[3:] = -1.0
    head_sel = np.repeat(np.eye(NH, dtype=np.float32), HS, 0)
    exp_sel = np.zeros((3, NE, 16, P), np.float32)
    for e in range(NE):
        exp_sel[:, e, e // 2, 64 * (e % 2):64 * (e % 2) + 64] = 1.0
    return {
        "x": d["L0_attn_x"], "w_qkv": d["L0_attn_W_attn"].T, "w_proj": d["L0_attn_W_proj"].T,
        "gate": d["L0_ffn_gate_w"].T, "e_bias": d["L0_ffn_e_bias"], "up": up.T, "down": down,
        "ident": np.eye(P, dtype=np.float32), "head_sel": head_sel,
        "q_stair": q_stair.astype(b16), "k_stair": k_stair.astype(b16), "q_rows": q_rows.astype(b16),
        "k_rows": k_rows.astype(b16),
        "exp_sel": exp_sel.reshape(3 * NE, 16, P).astype(b16),
    }


def kernel(**inputs):
    import numpy as _np
    import concourse.bacc as _bacc
    from concourse import mybir as _mybir
    from concourse.bass_utils import run_bass_kernel_spmd as _run

    nc = _bacc.Bacc("TRN2", target_bir_lowering=False, num_devices=1)
    laid = layout(inputs)
    arrays, args = {}, []
    for name in _INS:
        a = _np.ascontiguousarray(laid[name])
        arrays[f"in_{name}_dram"] = a
        args.append(nc.dram_tensor(f"in_{name}_dram", a.shape, _mybir.dt.from_np(a.dtype), kind="ExternalInput").ap())
    args.append(nc.dram_tensor("out_0_dram", (B, T, C), _mybir.dt.float32, kind="ExternalOutput").ap())
    build(nc, *args)
    r = _run(nc, [arrays], core_ids=[0])
    return r.results[0]["out_0_dram"]
```
